# Optimizing a Trainium2 kernel written in Bass

```python
import numpy as np
import jax
import jax.numpy as jnp

def _softmax(x, axis=-1):
    return jax.nn.softmax(x, axis=axis)

def _gelu(x):
    return jax.nn.gelu(x, approximate=True)

def _silu(x):
    return jax.nn.silu(x)

def _sigmoid(x):
    return jax.nn.sigmoid(x)

def _layernorm(x, axis=-1, eps=1e-05):
    m = jnp.mean(x, axis=axis, keepdims=True)
    v = jnp.var(x, axis=axis, keepdims=True)
    return (x - m) / jnp.sqrt(v + eps)

def _scatter_add(tgt, idx, src, axis=0):
    return tgt.at[idx].add(src)

def _segment_sum(src, seg, n):
    return jax.ops.segment_sum(src, seg, n)
kernel_name = 'mk_early_fusion_d1_tok_img256_r4_e6c5da'

def setup_inputs(seed: int=0):
    np.random.seed(seed)
    _w = jnp.asarray

    def _rec_inputs():
        import jax
        import jax.numpy as jnp
        _rk = jax.random.key(seed)
        x = -7.10856e-05 + 0.999911 * jax.random.normal(jax.random.fold_in(_rk, 1), (8, 64, 64, 64), jnp.float32)
        txt = -0.000490742 + 0.125618 * jax.random.normal(jax.random.fold_in(_rk, 2), (8, 128, 64), jnp.float32)
        return (x, txt)
    x, txt = _rec_inputs()

    def _L0_tok_setup():
        import jax, jax.numpy as jnp
        import numpy as np
        GS = 8
        NH = 8
        DM = 64
        B, W, H = (4, 64, 64)
        key = jax.random.key(seed)
        ks = jax.random.split(key, 5)
        s = 0.02
        return {'x': jax.random.normal(ks[0], (B, DM, W, H), dtype=jnp.float32), 'Wq': jax.random.normal(ks[1], (DM, DM), dtype=jnp.float32) * s, 'bq': jnp.zeros((DM,), dtype=jnp.float32), 'Wk': jax.random.normal(ks[2], (DM, DM), dtype=jnp.float32) * s, 'bk': jnp.zeros((DM,), dtype=jnp.float32), 'Wv': jax.random.normal(ks[3], (DM, DM), dtype=jnp.float32) * s, 'bv': jnp.zeros((DM,), dtype=jnp.float32), 'Wo': jax.random.normal(ks[4], (DM, DM), dtype=jnp.float32) * s, 'bo': jnp.zeros((DM,), dtype=jnp.float32)}
    _L0_tok_all = _L0_tok_setup()
    _L0_tok_in = {k: v for k, v in _L0_tok_all.items() if k in ('Wq', 'bq', 'Wk', 'bk', 'Wv', 'bv', 'Wo', 'bo')}
    del _L0_tok_all

    def _L0_attn_setup():
        import jax, jax.numpy as jnp
        import numpy as np
        import math
        EMBED_DIM = 64
        SEQ_LEN = 1024
        BATCH = 4
        NUM_SCALES = (24.0, 720.0)
        key = jax.random.key(seed)
        ks = jax.random.split(key, 8)
        d = EMBED_DIM
        x = jax.random.normal(ks[0], (BATCH, SEQ_LEN, d), dtype=jnp.float32)
        s = 1.0 / math.sqrt(d)
        Wq = jax.random.uniform(ks[1], (d, d), jnp.float32, -s, s)
        bq = jax.random.uniform(ks[2], (d,), jnp.float32, -s, s)
        Wk = jax.random.uniform(ks[3], (d, d), jnp.float32, -s, s)
        bk = jax.random.uniform(ks[4], (d,), jnp.float32, -s, s)
        Wv = jax.random.uniform(ks[5], (d, d), jnp.float32, -s, s)
        bv = jax.random.uniform(ks[6], (d,), jnp.float32, -s, s)
        beta = jnp.ones((len(NUM_SCALES),), dtype=jnp.float32)
        return {'x': x, 'Wq': Wq, 'bq': bq, 'Wk': Wk, 'bk': bk, 'Wv': Wv, 'bv': bv, 'beta': beta}
    _L0_attn_all = _L0_attn_setup()
    _L0_attn_in = {k: v for k, v in _L0_attn_all.items() if k in ('Wq', 'bq', 'Wk', 'bk', 'Wv', 'bv', 'beta')}
    del _L0_attn_all

    def _L0_ffn_setup():
        import jax, jax.numpy as jnp
        import numpy as np
        B, T, IN_DIM = (64, 64, 64)
        HID, OUT_DIM = (128, 64)
        N_LAYERS, N_EXPERTS, N_SHARED = (2, 16, 1)
        key = jax.random.key(seed)
        ks = jax.random.split(key, 10)
        s = 0.02
        x = jax.random.normal(ks[0], (B, T, IN_DIM), dtype=jnp.float32)
        route_id = jax.random.randint(ks[1], (B,), 0, N_EXPERTS)
        Wi = jax.random.normal(ks[2], (HID, IN_DIM), dtype=jnp.float32) * s
        bi = jnp.zeros((HID,), dtype=jnp.float32)
        Wr = jax.random.normal(ks[3], (N_LAYERS, N_EXPERTS, HID, HID), dtype=jnp.float32) * s
        br = jax.random.normal(ks[4], (N_LAYERS, N_EXPERTS, HID), dtype=jnp.float32) * s
        Ws = jax.random.normal(ks[5], (N_LAYERS, N_SHARED, HID, HID), dtype=jnp.float32) * s
        bs = jax.random.normal(ks[6], (N_LAYERS, N_SHARED, HID), dtype=jnp.float32) * s
        Wo = jax.random.normal(ks[7], (OUT_DIM, HID), dtype=jnp.float32) * s
        bo = jnp.zeros((OUT_DIM,), dtype=jnp.float32)
        return {'x': x, 'route_id': route_id, 'Wi': Wi, 'bi': bi, 'Wr': Wr, 'br': br, 'Ws': Ws, 'bs': bs, 'Wo': Wo, 'bo': bo}
    _L0_ffn_all = _L0_ffn_setup()
    _L0_ffn_in = {k: v for k, v in _L0_ffn_all.items() if k in ('route_id', 'Wi', 'bi', 'Wr', 'br', 'Ws', 'bs', 'Wo', 'bo')}
    del _L0_ffn_all
    return {'x': x, 'txt': txt, 'L0_tok_Wq': _L0_tok_in['Wq'], 'L0_tok_bq': _L0_tok_in['bq'], 'L0_tok_Wk': _L0_tok_in['Wk'], 'L0_tok_bk': _L0_tok_in['bk'], 'L0_tok_Wv': _L0_tok_in['Wv'], 'L0_tok_bv': _L0_tok_in['bv'], 'L0_tok_Wo': _L0_tok_in['Wo'], 'L0_tok_bo': _L0_tok_in['bo'], 'L0_attn_Wq': _L0_attn_in['Wq'], 'L0_attn_bq': _L0_attn_in['bq'], 'L0_attn_Wk': _L0_attn_in['Wk'], 'L0_attn_bk': _L0_attn_in['bk'], 'L0_attn_Wv': _L0_attn_in['Wv'], 'L0_attn_bv': _L0_attn_in['bv'], 'L0_attn_beta': _L0_attn_in['beta'], 'L0_ffn_route_id': _L0_ffn_in['route_id'], 'L0_ffn_Wi': _L0_ffn_in['Wi'], 'L0_ffn_bi': _L0_ffn_in['bi'], 'L0_ffn_Wr': _L0_ffn_in['Wr'], 'L0_ffn_br': _L0_ffn_in['br'], 'L0_ffn_Ws': _L0_ffn_in['Ws'], 'L0_ffn_bs': _L0_ffn_in['bs'], 'L0_ffn_Wo': _L0_ffn_in['Wo'], 'L0_ffn_bo': _L0_ffn_in['bo']}

def reference(x, txt, L0_tok_Wq, L0_tok_bq, L0_tok_Wk, L0_tok_bk, L0_tok_Wv, L0_tok_bv, L0_tok_Wo, L0_tok_bo, L0_attn_Wq, L0_attn_bq, L0_attn_Wk, L0_attn_bk, L0_attn_Wv, L0_attn_bv, L0_attn_beta, L0_ffn_route_id, L0_ffn_Wi, L0_ffn_bi, L0_ffn_Wr, L0_ffn_br, L0_ffn_Ws, L0_ffn_bs, L0_ffn_Wo, L0_ffn_bo):
    import jax
    import jax.numpy as jnp

    def _L0_tok_ref(x, Wq, bq, Wk, bk, Wv, bv, Wo, bo):
        import jax, jax.numpy as jnp
        import numpy as np
        GS = 8
        NH = 8
        DM = 64
        B, W, H = (4, 64, 64)
        b, d, w, h = x.shape
        gw, gh = (w // GS, h // GS)
        n = gw * gh
        L = GS * GS
        dh = d // NH
        q = x.reshape(b, d, gw, GS, gh, GS).mean(axis=(3, 5))
        q = q.reshape(b, d, n).transpose(0, 2, 1).reshape(b * n, 1, d)
        kv = x.transpose(0, 2, 3, 1)
        kv = kv.reshape(b, gw, GS, gh, GS, d)
        kv = kv.transpose(0, 1, 3, 2, 4, 5).reshape(b * n, L, d)
        qp = (q @ Wq.T + bq).reshape(b * n, 1, NH, dh).transpose(0, 2, 1, 3)
        kp = (kv @ Wk.T + bk).reshape(b * n, L, NH, dh).transpose(0, 2, 1, 3)
        vp = (kv @ Wv.T + bv).reshape(b * n, L, NH, dh).transpose(0, 2, 1, 3)
        scores = jnp.einsum('bhqd,bhkd->bhqk', qp, kp) / jnp.sqrt(jnp.float32(dh))
        attn = jax.nn.softmax(scores, axis=-1)
        ctx = jnp.einsum('bhqk,bhkd->bhqd', attn, vp)
        ctx = ctx.transpose(0, 2, 1, 3).reshape(b * n, 1, d)
        attn_out = ctx @ Wo.T + bo
        out = q + attn_out
        return out.reshape(b, n, d)

    def _L0_attn_ref(x, Wq, bq, Wk, bk, Wv, bv, beta):
        import jax, jax.numpy as jnp
        import numpy as np
        import math
        EMBED_DIM = 64
        SEQ_LEN = 1024
        BATCH = 4
        NUM_SCALES = (24.0, 720.0)
        d = x.shape[-1]
        seq_len = x.shape[1]
        sqrt_d = jnp.asarray(math.sqrt(d), x.dtype)
        Q = jnp.einsum('bsd,ed->bse', x, Wq) + bq
        K = jnp.einsum('bsd,ed->bse', x, Wk) + bk
        V = jnp.einsum('bsd,ed->bse', x, Wv) + bv
        attn = jnp.einsum('bse,bte->bst', Q, K) / sqrt_d
        idx = jnp.arange(seq_len, dtype=jnp.float32)
        absdiff = jnp.abs(idx[:, None] - idx[None, :])
        two_pi = jnp.asarray(2.0 * math.pi, jnp.float32)
        bias = jnp.zeros((seq_len, seq_len), dtype=jnp.float32)
        for n, T in enumerate(NUM_SCALES):
            bias = bias + beta[n] * jnp.cos(two_pi * absdiff / T)
        scores = jax.nn.softmax(attn + bias[None, :, :], axis=-1)
        return jnp.einsum('bst,bte->bse', scores, V)

    def _L0_ffn_ref(x, route_id, Wi, bi, Wr, br, Ws, bs, Wo, bo):
        import jax, jax.numpy as jnp
        import numpy as np
        B, T, IN_DIM = (64, 64, 64)
        HID, OUT_DIM = (128, 64)
        N_LAYERS, N_EXPERTS, N_SHARED = (2, 16, 1)
        flat = x.reshape(-1, x.shape[-1])
        n_tok = flat.shape[0]
        route = jnp.repeat(route_id, n_tok // route_id.shape[0])
        h = jax.nn.relu(flat @ Wi.T + bi)
        n_layers, n_experts = (Wr.shape[0], Wr.shape[1])
        for l in range(n_layers):
            shared = (jnp.einsum('nd,shd->snh', h, Ws[l]) + bs[l][:, None, :]).mean(axis=0)
            routed = jnp.zeros_like(h)
            for e in range(n_experts):
                ye = h @ Wr[l, e].T + br[l, e]
                routed = routed + jnp.where((route == e)[:, None], ye, 0.0)
            h = jax.nn.relu(shared + routed + h)
        out = h @ Wo.T + bo
        return out.reshape(*x.shape[:-1], out.shape[-1])
    h = _L0_tok_ref(x, L0_tok_Wq, L0_tok_bq, L0_tok_Wk, L0_tok_bk, L0_tok_Wv, L0_tok_bv, L0_tok_Wo, L0_tok_bo)
    h = jnp.concatenate([h, txt], axis=1)
    h = h + _L0_attn_ref(_layernorm(h, axis=-1), L0_attn_Wq, L0_attn_bq, L0_attn_Wk, L0_attn_bk, L0_attn_Wv, L0_attn_bv, L0_attn_beta)
    h = h + _L0_ffn_ref(_layernorm(h, axis=-1), L0_ffn_route_id, L0_ffn_Wi, L0_ffn_bi, L0_ffn_Wr, L0_ffn_br, L0_ffn_Ws, L0_ffn_bs, L0_ffn_Wo, L0_ffn_bo)
    return h

_drawn_inputs = setup_inputs


def setup_inputs(seed=0):
    import zlib

    import numpy as np

    out = dict(_drawn_inputs(seed))
    spreads = {'L0_tok_bq': (0.0, 0.8),
     'L0_tok_bk': (0.0, 2.0),
     'L0_tok_bv': (0.0, 0.1),
     'L0_tok_bo': (0.0, 0.1),
     'L0_attn_beta': (1.0, 0.6),
     'L0_ffn_bi': (0.0, 0.1),
     'L0_ffn_bo': (0.0, 0.1)}
    factors = {'L0_tok_Wq': 21.335, 'L0_tok_Wk': 8.0, 'L0_tok_Wv': 6.571, 'L0_attn_bk': 64.0}
    for name, (base, spread) in spreads.items():
        noise = np.random.default_rng([zlib.crc32(name.encode()), seed]).standard_normal(out[name].shape)
        drawn = base * np.exp(spread * noise) if base else spread * noise
        out[name] = jnp.asarray(drawn.astype(out[name].dtype))
    for name, factor in factors.items():
        out[name] = (out[name] * factor).astype(out[name].dtype)
    return out
```

```python
from contextlib import ExitStack

import concourse.bass as bass
from concourse import mybir

F32 = mybir.dt.float32
I32 = mybir.dt.int32
ALU = mybir.AluOpType
ACT = mybir.ActivationFunctionType
AX = mybir.AxisListType.X

P = 128
D = 64
NH, DH = 8, 8
B = 8
C = B // 2
G = 64
PIX = 64
QUART = 16
SLICE = 8
SLOT = 2 * NH
COLT = 32
TXT = 128
T = G + TXT
TT = T // 2
HID = 128
NE = 16
NL = 2
RG = B * T // 64
GC = 2 * T // RG
LN_EPS = 1e-5

W8 = dict(wq=(0, NH * P), wk=(NH * P, NH * P), wv=(2 * NH * P, NH * P), wo=(3 * NH * P, NH * D),
          bq=(3 * NH * P + NH * D, NH), bk=(3 * NH * P + NH * D + NH, NH))
W8_N = 3 * NH * P + NH * D + 2 * NH


def _columns(parts):
    at, out = 0, {}
    for name, n in parts:
        out[name] = (at, n)
        at += n
    return out, at


EARLY, EARLY_N = _columns([("woT", P), ("bv", 1), ("bo", 1), ("bqr", DH), ("bkr", DH), ("mask", NH)])
MID, MID_N = _columns([
    ("ident", P), ("center", P), ("mean", P), ("wqT", P), ("wkT", P), ("wvT", P), ("bq", 1), ("bk", 1),
    ("bv", 1), ("wiT", 2 * P), ("bi", 1), ("woT", D), ("bo", 1), ("brs", NL * HID), ("expert", 1),
    ("shared", 1), ("beta", 2), ("cos", 2 * 2 * T), ("wsT", NL * HID)])


def early_fusion_kernel(nc: bass.Bass, x_ch, x_px, txt, w8_d, early_d, mid_d, wrT_d, route_d, out):
    with ExitStack() as ctx:
        def sb(name, shape, dt=F32):
            return ctx.enter_context(nc.sbuf_tensor(name, shape, dt))

        def sem(name):
            return ctx.enter_context(nc.semaphore(name))

        xch = sb("xch", [P, 3, G * PIX])
        xpx = sb("xpx", [P, 2, G // 2, P])
        early = sb("early", [P, EARLY_N])
        mid = sb("mid", [P, MID_N])
        wrT = sb("wrT", [P, NL, NE, HID])
        sel = sb("sel", [P, 2, GC, NL, HID])
        w8 = sel[0:DH, 1].rearrange("d g l n -> d (g l n)")[:, 0:W8_N]
        wsI = sb("wsI", [P, NL, HID])
        route = sb("route", [P, 64], I32)
        onehot = sb("onehot", [P, 64])
        MT = sb("MT", [P, NH, P])
        AO = sb("AO", [P, NH, P])
        tq = sb("tq", [P, NH])
        Bk = sb("Bk", [P, NH, 2, NH])
        bqk = sb("bqk", [P, DH])
        cst = sb("cst", [P, 1])
        boo = sb("boo", [P, 1])
        epsc = sb("epsc", [P, 1])
        cosb = sb("cosb", [P, 2, T])
        qsum = sb("qsum", [P, 2, G])
        qm = sb("qm", [P, 2, G])
        R = sb("R", [P, 2, G, COLT])
        ck = sb("ck", [P, G])
        ck2 = sb("ck2", [P, 8])
        cc = sb("cc", [P, 8])
        mx = sb("mx", [P, 8])
        sh = sb("sh", [P, 8])
        nsh = sb("nsh", [P, 8])
        E = sb("E", [P, 8, PIX])
        den = sb("den", [P, 8])
        rden = sb("rden", [P, 8])
        AT = sb("AT", [P, G // 2, 2, 2, NH])
        Z = sb("Z", [P, NH, G // 2, 2])
        h = sb("h", [P, C, T])
        h2 = sb("h2", [P, 2, T])
        sq = sb("sq", [P, T])
        lv = sb("lv", [P, T])
        rstd = sb("rstd", [P, T])
        xn = sb("xn", [P, T])
        QT = sb("QT", [P, T])
        KT = sb("KT", [P, T])
        V = sb("V", [TT, 2, P])
        Pr = sb("Pr", [TT, 2, 2, T])
        nmx = sb("nmx", [TT, 4])
        pden = sb("pden", [TT, 4])
        prden = sb("prden", [TT, 4])
        PT = sb("PT", [TT, 2, 2, T])
        hid = sb("hid", [P, NL + 1, 2 * T])
        outT = sb("outT", [P, C, T])

        bank = [ctx.enter_context(nc.psum_tensor(f"bank{i}", [P, 512], F32)) for i in range(8)]
        bS = [bank[0], bank[1]]
        bRT = bank[2]
        bZ = [bank[3], bank[4]]
        b5, b6, b7 = bank[5], bank[6], bank[7]

        x_ch_in = [[sem(f"x_ch_in{c}_{k}") for k in range(4)] for c in range(C)]
        x_px_in = [[sem(f"x_px_in{c}_{k}") for k in range(2)] for c in range(C)]
        txt_in = [sem(f"txt_in{c}") for c in range(C)]
        w8_in, early_in, mid_in, wr_in, route_in = (sem(n) for n in ("w8_in", "early_in", "mid_in", "wr_in", "route_in"))
        out_stored = [sem(f"out_stored{c}") for c in range(C)]
        dve_zeroed, pool_zeroed, products_made, ao_ready, consts_ready = (
            sem(n) for n in ("dve_zeroed", "pool_zeroed", "products_made", "ao_ready", "consts_ready"))
        mid_consts_ready, bias_part, wsi_ready, group_selected = (
            sem(n) for n in ("mid_consts_ready", "bias_part", "wsi_ready", "group_selected"))
        qsum_ready, q_ready, r_ready, r_copied, ck_masked, cc_part, cc_ready = (
            sem(n) for n in ("qsum_ready", "q_ready", "r_ready", "r_copied", "ck_masked", "cc_part", "cc_ready"))
        scores_ready, mx_ready, sh_ready, nsh_ready, shifted, exp_ready = (
            sem(n) for n in ("scores_ready", "mx_ready", "sh_ready", "nsh_ready", "shifted", "exp_ready"))
        den_ready, rden_ready, attn_ready, attnT_ready, at_lo_copied, at_hi_copied = (
            sem(n) for n in ("den_ready", "rden_ready", "attn_ready", "attnT_ready", "at_lo_copied", "at_hi_copied"))
        z_ready, z_lo_copied, z_hi_copied, tok_ready, h_ready = (
            sem(n) for n in ("z_ready", "z_lo_copied", "z_hi_copied", "tok_ready", "h_ready"))
        xc_ready, sq_ready, var_ready, lv_ready, rstd_ready, xn_ready = (
            sem(n) for n in ("xc_ready", "sq_ready", "var_ready", "lv_ready", "rstd_ready", "xn_ready"))
        qk_ready, v_ready, q_copied, k_copied, v_copied, s_ready, biased, pexp_ready = (
            sem(n) for n in ("qk_ready", "v_ready", "q_copied", "k_copied", "v_copied", "s_ready", "biased", "pexp_ready"))
        prden_ready, p_ready, pt_ready, pt0_copied, pt1_copied, pv_ready, h2_ready = (
            sem(n) for n in ("prden_ready", "p_ready", "pt_ready", "pt0_copied", "pt1_copied", "pv_ready", "h2_ready"))
        hid_ready, hid_relued, wo_ready, out_ready = (sem(n) for n in ("hid_ready", "hid_relued", "wo_ready", "out_ready"))

        def w(name, rows=slice(0, DH)):
            at, n = W8[name]
            return w8[rows, at:at + n]

        def e(name, rows=slice(0, P)):
            at, n = EARLY[name]
            return early[rows, at:at + n]

        def m(name, rows=slice(0, P)):
            at, n = MID[name]
            return mid[rows, at:at + n]

        HALF = [slice(0, D), slice(D, P)]
        INV = float(DH) ** -0.5
        wq8 = w("wq").rearrange("d (h n) -> d h n", h=NH)
        wk8 = w("wk").rearrange("d (h n) -> d h n", h=NH)
        wv8 = w("wv").rearrange("d (h n) -> d h n", h=NH)
        wo8 = w("wo").rearrange("d (h n) -> d h n", h=NH)
        wiT = m("wiT").rearrange("p (f n) -> p f n", f=2)
        brs = m("brs").rearrange("p (l n) -> p l n", l=NL)
        wsT = m("wsT").rearrange("p (l n) -> p l n", l=NL)
        cos = m("cos").rearrange("p (n a t) -> p n a t", n=2, a=2)

        def interval(c):
            a, b, p = c, c + 1, c + 2
            order = [
                ("scores", b, 0), ("ln_center", a, 0), ("pool", p, 0), ("scores", b, 1), ("scores", b, 2),
                ("ln_var", a, 0), ("pool", p, 1), ("scores", b, 3), ("scores", b, 4), ("scores", b, 5),
                ("qkv", a, 0), ("scores", b, 6), ("scores", b, 7), ("attn_scores", a, 0), ("shift", b, 0),
                ("attn_norm", a, 0), ("attn_turn", a, 0), ("attn_apply", a, 0), ("normalise", b, 0),
                ("ln_center", a, 1), ("turn", b, 0), ("ln_var", a, 1), ("z", b, 0), ("z", b, 1),
                ("expand", a, 0), ("z", b, 2), ("pool", p, 2), ("experts", a, 0), ("z", b, 3), ("pool", p, 3),
                ("experts", a, 1), ("tokens", b, 0), ("query", p, 0), ("project", a, 0)]
            return [s for s in order if 0 <= s[1] < C]

        SCHEDULE = [("pool", 0, k) for k in range(4)] + [("query", 0, 0)]
        for c in range(-1, C):
            SCHEDULE += interval(c)

        block = ctx.enter_context(nc.Block())

        @block.sync
        def _(sp):
            def load_ch(c):
                if c >= 3:
                    sp.wait_ge(scores_ready, c - 2)
                for k in range(4):
                    cols = slice(k * QUART * PIX, (k + 1) * QUART * PIX)
                    sp.dma_start(xch[:, c % 3, cols], x_ch[c, :, cols]).then_inc(x_ch_in[c][k], 16)

            def load_px(c):
                if c >= 2:
                    sp.wait_ge(z_ready, 2 * (c - 1))
                for k in range(2):
                    gp = slice(k * G // 4, (k + 1) * G // 4)
                    sp.dma_start(xpx[:, c % 2, gp, :], x_px[c, :, gp, :]).then_inc(x_px_in[c][k], 16)

            load_ch(0)
            sp.dma_start(route[:], route_d).then_inc(route_in, 16)
            load_px(0)
            sp.dma_start(mid[:], mid_d).then_inc(mid_in, 16)
            load_ch(1)
            sp.dma_start(wrT[:], wrT_d).then_inc(wr_in, 16)
            for c in range(C):
                sp.dma_start(h[:, c, G:T], txt[c]).then_inc(txt_in[c], 16)
            load_px(1)
            load_ch(2)
            load_ch(3)
            load_px(2)
            load_px(3)
            for c in range(C):
                sp.wait_ge(out_ready, c + 1)
                sp.dma_start(out[c], outT[:, c, :]).then_inc(out_stored[c], 16)
            for c in range(C):
                sp.wait_ge(out_stored[c], 16)

        @block.gpsimd
        def _(pool):
            pool.memset(AO[:], 0.0).then_inc(pool_zeroed, 1)
            pool.memset(AT[:], 0.0).then_inc(pool_zeroed, 1)
            pool.memset(R[:, 1], 0.0).then_inc(pool_zeroed, 1)
            pool.wait_ge(mid_in, 16)
            for l in range(NL):
                pool.tensor_tensor(wsI[:, l, :], wsT[:, l, :], m("ident"), ALU.add).then_inc(wsi_ready, 1)
            pool.wait_ge(wsi_ready, NL)
            pool.wait_ge(wr_in, 16)
            pool.wait_ge(route_in, 16)
            pool.wait_ge(products_made, 1)
            for c in range(C):
                if c >= 2:
                    pool.wait_ge(hid_ready, 3 * (c - 1))
                with pool.Fori(0, GC) as g:
                    ex = pool.value_load(route[0:1, bass.ds(g + GC * c, 1)], min_val=0, max_val=NE - 1)
                    for l in range(NL):
                        pool.tensor_tensor(sel[:, c % 2, bass.ds(g, 1), l, :], wrT[:, l, bass.ds(ex, 1), :],
                                           wsI[:, l:l + 1, :], ALU.add).then_inc(group_selected, 1)

        @block.scalar
        def _(act):
            act.dma_start(w8, w8_d).then_inc(w8_in, 16)
            act.dma_start(early[:], early_d).then_inc(early_in, 16)
            act.wait_ge(pool_zeroed, 1)
            act.wait_ge(products_made, 1)
            for f in range(2):
                act.activation(AO[HALF[f], :, f * D:(f + 1) * D],
                               bank[1][HALF[f], :].rearrange("p (h n) -> p h n", h=NH),
                               ACT.Copy).then_inc(ao_ready, 1)

            for step, c, k in SCHEDULE:
                ln = 2 * c + k
                if step == "shift":
                    act.wait_ge(shifted, c + 1)
                    act.activation(E[:], E[:], ACT.Exp).then_inc(exp_ready, 1)
                elif step == "turn":
                    act.wait_ge(attnT_ready, c + 1)
                    if c == 0:
                        act.wait_ge(pool_zeroed, 2)
                    if c > 0:
                        act.wait_ge(z_ready, 2 * c)
                    act.activation(AT[HALF[0], :, :, 0, :],
                                   bRT[HALF[0], :].rearrange("p (g f h) -> p g f h", f=2, h=NH),
                                   ACT.Copy).then_inc(at_lo_copied, 1)
                elif step == "z" and k % 2:
                    n = k // 2
                    act.wait_ge(z_ready, 2 * c + n + 1)
                    if c > 0:
                        act.wait_ge(tok_ready, c)
                    act.activation(Z[HALF[0], :, 16 * n:16 * n + 16, :].rearrange("p h g s -> p g s h"),
                                   bZ[n][HALF[0], :].rearrange("p (g f s h) -> p g f s h", f=2, s=2, h=NH)[:, :, 0],
                                   ACT.Copy).then_inc(z_lo_copied, 1)
                elif step == "ln_center":
                    act.wait_ge(xc_ready, ln + 1)
                    act.activation(sq[:], (b5 if k == 0 else b5)[:, 0:T], ACT.Square).then_inc(sq_ready, 1)
                elif step == "ln_var":
                    act.wait_ge(var_ready, ln + 1)
                    if ln == 0:
                        act.wait_ge(dve_zeroed, 2)
                    act.activation(lv[:], b6[:, 0:T], ACT.Ln, bias=epsc[:, 0:1]).then_inc(lv_ready, 1)
                    act.wait_ge(lv_ready, ln + 1)
                    if ln > 0:
                        act.wait_ge(xn_ready, ln)
                    act.activation(rstd[:], lv[:], ACT.Exp, scale=-0.5).then_inc(rstd_ready, 1)
                elif step == "qkv":
                    act.wait_ge(qk_ready, c + 1)
                    act.activation(KT[:], b7[:, 0:T], ACT.Identity, bias=m("bk")).then_inc(k_copied, 1)
                    act.wait_ge(v_ready, c + 1)
                    act.activation(V[:], b5[0:TT, 0:2 * P].rearrange("p (a n) -> p a n", a=2),
                                   ACT.Copy).then_inc(v_copied, 1)
                elif step == "attn_scores":
                    for i in range(4):
                        act.wait_ge(biased, 4 * c + i + 1)
                        act.activation(Pr[:, i // 2, i % 2, :], Pr[:, i // 2, i % 2, :], ACT.Exp,
                                       bias=nmx[:, i:i + 1], scale=-1.0,
                                       accum_out=pden[:, i:i + 1]).then_inc(pexp_ready, 1)
                elif step == "attn_turn":
                    act.wait_ge(pt_ready, 2 * c + 1)
                    act.activation(PT[:, 0], b5[0:TT, 0:2 * T].rearrange("p (a t) -> p a t", a=2),
                                   ACT.Copy).then_inc(pt0_copied, 1)
                elif step == "expand":
                    act.wait_ge(hid_ready, 3 * c + 1)
                    act.activation(hid[:, 0, :], b7[:, 0:2 * T], ACT.Relu, bias=m("bi")).then_inc(hid_relued, 1)
                elif step == "experts":
                    act.wait_ge(hid_ready, 3 * c + 2 + k)
                    act.activation(hid[:, k + 1, :], [b5, b6][k][:, 0:2 * T], ACT.Relu).then_inc(hid_relued, 1)

        @block.vector
        def _(dve):
            dve.memset(MT[:], 0.0).then_inc(dve_zeroed, 1)
            dve.memset(epsc[:], LN_EPS).then_inc(dve_zeroed, 1)
            dve.memset(Bk[:], 0.0).then_inc(dve_zeroed, 1)
            dve.memset(R[:, 0], 0.0).then_inc(dve_zeroed, 1)
            dve.wait_ge(early_in, 16)
            dve.tensor_tensor(bqk[:], e("bqr"), e("bkr"), ALU.mult).then_inc(bias_part, 1)
            dve.wait_ge(products_made, 1)
            dve.wait_ge(dve_zeroed, 4)
            for f in range(2):
                dve.tensor_scalar(MT[HALF[f], :, f * D:(f + 1) * D],
                                  bank[0][HALF[f], :].rearrange("p (h n) -> p h n", h=NH),
                                  INV, None, ALU.mult).then_inc(consts_ready, 1)
                dve.tensor_scalar(Bk[HALF[f], :, f, :],
                                  bank[3][HALF[f], 0:NH].rearrange("p (o h) -> p o h", o=1).to_broadcast([D, NH, NH]),
                                  INV, None, ALU.mult).then_inc(consts_ready, 1)
            dve.tensor_scalar(tq[:], bank[2][:, 0:NH], INV, None, ALU.mult).then_inc(consts_ready, 1)
            dve.tensor_tensor(boo[:], bank[4][:, 0:1], e("bo"), ALU.add).then_inc(consts_ready, 1)
            dve.wait_ge(bias_part, 1)
            dve.tensor_reduce(cst[:], bqk[:], AX, ALU.add).then_inc(bias_part, 1)
            dve.wait_ge(bias_part, 2)
            dve.tensor_scalar(cst[:], cst[:], INV, None, ALU.mult).then_inc(consts_ready, 1)

            def mid_consts():
                dve.wait_ge(mid_in, 16)
                dve.wait_ge(route_in, 16)
                dve.tensor_scalar(onehot[:], route[:], m("expert"), m("shared"), ALU.is_equal,
                                  ALU.add).then_inc(mid_consts_ready, 1)
                dve.tensor_scalar(cosb[0:TT], cos[0:TT, 0], m("beta")[0:TT, 0:1], None, ALU.mult).then_inc(bias_part, 1)
                dve.wait_ge(bias_part, 3)
                dve.scalar_tensor_tensor(out=cosb[0:TT], in0=cos[0:TT, 1], scalar=m("beta")[0:TT, 1:2], in1=cosb[0:TT],
                                         op0=ALU.mult, op1=ALU.add).then_inc(mid_consts_ready, 1)

            for step, c, k in SCHEDULE:
                ln = 2 * c + k
                if step == "pool":
                    dve.wait_ge(x_ch_in[c][k], 16)
                    dve.tensor_reduce(qsum[:, c % 2, QUART * k:QUART * (k + 1)],
                                      xch[:, c % 3, QUART * PIX * k:QUART * PIX * (k + 1)]
                                      .rearrange("p (g n) -> p g n", n=PIX), AX, ALU.add).then_inc(qsum_ready, 1)
                elif step == "query":
                    dve.wait_ge(qsum_ready, 4 * (c + 1))
                    dve.tensor_scalar(qm[:, c % 2, :], qsum[:, c % 2, :], 1.0 / PIX, None, ALU.mult).then_inc(q_ready, 1)
                    if c == 0:
                        dve.wait_ge(consts_ready, 7)
                    if c == 1:
                        dve.wait_ge(pool_zeroed, 3)
                    dve.wait_ge(r_ready, c + 1)
                    rp = bRT[:].rearrange("p (h m k s) -> p h m k s", h=NH, k=2, s=2)
                    rs = R[:, c % 2].rearrange("p (m k s) n -> p m k s n", k=2, s=2)
                    for f in range(2):
                        for slot in range(2):
                            at = SLOT * slot + NH * f
                            dve.tensor_tensor(
                                rs[HALF[f], :, slot, :, at:at + NH].rearrange("p m s h -> p h m s"),
                                rp[HALF[f], :, :, slot, :],
                                tq[HALF[f], :].rearrange("p (h o q) -> p h o q", o=1, q=1).to_broadcast([D, NH, 16, 2]),
                                ALU.add).then_inc(r_copied, 1)
                    dve.tensor_tensor(ck[:].rearrange("p (q n s) -> p q n s", q=4, s=2),
                                      bZ[1][:, 0:G].rearrange("p (q n s) -> p q n s", q=4, s=2),
                                      e("mask").rearrange("p (o n q) -> p o n q", o=1, q=1).to_broadcast([P, 4, NH, 2]),
                                      ALU.mult).then_inc(ck_masked, 1)
                    dve.wait_ge(ck_masked, c + 1)
                    dve.tensor_reduce(ck2[:].rearrange("p (q s) -> p q s", s=2),
                                      ck[:].rearrange("p (q n s) -> p q s n", q=4, s=2), AX, ALU.add).then_inc(cc_part, 1)
                    dve.wait_ge(cc_part, c + 1)
                    dve.tensor_scalar(cc[:], ck2[:], cst[:, 0:1], None, ALU.add).then_inc(cc_ready, 1)
                elif step == "shift":
                    if c == 0:
                        mid_consts()
                    S = bS[c % 2][:].rearrange("p (s n) -> p s n", n=PIX)
                    dve.wait_ge(scores_ready, c + 1)
                    dve.tensor_reduce(mx[:], S, AX, ALU.max).then_inc(mx_ready, 1)
                    dve.wait_ge(mx_ready, c + 1)
                    dve.wait_ge(cc_ready, c + 1)
                    dve.tensor_tensor(sh[:], mx[:], cc[:], ALU.add).then_inc(sh_ready, 1)
                    dve.wait_ge(sh_ready, c + 1)
                    dve.tensor_tensor(nsh[:], cc[:], sh[:], ALU.subtract).then_inc(nsh_ready, 1)
                    dve.wait_ge(nsh_ready, c + 1)
                    if c > 0:
                        dve.wait_ge(attnT_ready, c)
                    dve.tensor_tensor(E[:], S, nsh[:].rearrange("p (s o) -> p s o", o=1).to_broadcast([P, 8, PIX]),
                                      ALU.add).then_inc(shifted, 1)
                elif step == "normalise":
                    dve.wait_ge(exp_ready, c + 1)
                    dve.tensor_reduce(den[:], E[:], AX, ALU.add).then_inc(den_ready, 1)
                    dve.wait_ge(den_ready, c + 1)
                    dve.reciprocal(rden[:], den[:]).then_inc(rden_ready, 1)
                    dve.wait_ge(rden_ready, c + 1)
                    dve.tensor_tensor(E[:], E[:], rden[:].rearrange("p (s o) -> p s o", o=1).to_broadcast([P, 8, PIX]),
                                      ALU.mult).then_inc(attn_ready, 1)
                elif step == "turn":
                    dve.wait_ge(attnT_ready, c + 1)
                    if c == 0:
                        dve.wait_ge(pool_zeroed, 2)
                    if c > 0:
                        dve.wait_ge(z_ready, 2 * c)
                    dve.tensor_copy(AT[HALF[1], :, :, 1, :],
                                    bRT[HALF[1], :].rearrange("p (g f h) -> p g f h", f=2, h=NH)).then_inc(at_hi_copied, 1)
                elif step == "z" and k % 2:
                    n = k // 2
                    dve.wait_ge(z_ready, 2 * c + n + 1)
                    if c > 0:
                        dve.wait_ge(tok_ready, c)
                    dve.tensor_copy(Z[HALF[1], :, 16 * n:16 * n + 16, :].rearrange("p h g s -> p g s h"),
                                    bZ[n][HALF[1], :].rearrange("p (g f s h) -> p g f s h", f=2, s=2, h=NH)[:, :, 1]
                                    ).then_inc(z_hi_copied, 1)
                elif step == "tokens":
                    dve.wait_ge(tok_ready, c + 1)
                    dve.scalar_tensor_tensor(out=h[:, c, 0:G], in0=bZ[0][:, 0:G], scalar=boo[:, 0:1], in1=qm[:, c % 2, :],
                                             op0=ALU.add, op1=ALU.add).then_inc(h_ready, 1)
                elif step == "ln_var":
                    dve.wait_ge(rstd_ready, ln + 1)
                    dve.tensor_tensor(xn[:], b5[:, 0:T], rstd[:], ALU.mult).then_inc(xn_ready, 1)
                elif step == "qkv":
                    dve.wait_ge(qk_ready, c + 1)
                    dve.tensor_scalar(QT[:], b6[:, 0:T], m("bq"), float(D) ** -0.5, ALU.add, ALU.mult).then_inc(q_copied, 1)
                elif step == "attn_scores":
                    for i in range(4):
                        f, s = i // 2, i % 2
                        dve.wait_ge(s_ready, 2 * c + f + 1)
                        if i == 0 and c == 0:
                            dve.wait_ge(mid_consts_ready, 2)
                        dve.tensor_tensor_reduce(Pr[:, f, s, :], [b6, b7][f][0:TT, s * T:(s + 1) * T], cosb[0:TT, s, :],
                                                 -1.0, 3.0e38, ALU.add, ALU.min, nmx[:, i:i + 1]).then_inc(biased, 1)
                elif step == "attn_norm":
                    dve.wait_ge(pexp_ready, 4 * (c + 1))
                    dve.reciprocal(prden[:], pden[:]).then_inc(prden_ready, 1)
                    dve.wait_ge(prden_ready, c + 1)
                    for i in range(4):
                        dve.tensor_scalar(Pr[:, i // 2, i % 2, :], Pr[:, i // 2, i % 2, :], prden[:, i:i + 1], None,
                                          ALU.mult).then_inc(p_ready, 1)
                elif step == "attn_turn":
                    dve.wait_ge(pt_ready, 2 * c + 2)
                    dve.tensor_copy(PT[:, 1], b6[0:TT, 0:2 * T].rearrange("p (a t) -> p a t", a=2)).then_inc(pt1_copied, 1)
                elif step == "attn_apply":
                    dve.wait_ge(pv_ready, c + 1)
                    dve.scalar_tensor_tensor(out=h2[:, c % 2, :], in0=b7[:, 0:T], scalar=m("bv"), in1=h[:, c, :],
                                             op0=ALU.add, op1=ALU.add).then_inc(h2_ready, 1)
                elif step == "project":
                    dve.wait_ge(wo_ready, c + 1)
                    dve.scalar_tensor_tensor(out=outT[:, c, :], in0=b7[:, 0:T], scalar=m("bo"), in1=h2[:, c % 2, :],
                                             op0=ALU.add, op1=ALU.add).then_inc(out_ready, 1)

        @block.tensor
        def _(pe):
            pe.wait_ge(w8_in, 16)
            pe.wait_ge(early_in, 16)
            for hd in range(NH):
                pe.matmul(bank[0][:, D * hd:D * (hd + 1)], wq8[:, hd, :], wk8[:, hd, 0:D], start=True, stop=True)
                pe.matmul(bank[1][:, D * hd:D * (hd + 1)], wv8[:, hd, :], wo8[:, hd, :], start=True, stop=True)
                pe.matmul(bank[2][:, hd:hd + 1], wk8[:, hd, :], w("bq")[:, hd:hd + 1], start=True, stop=True)
                pe.matmul(bank[3][:, hd:hd + 1], wq8[:, hd, :], w("bk")[:, hd:hd + 1], start=True, stop=True)
            pe.matmul(bank[4][:, 0:1], e("woT"), e("bv"), start=True, stop=True).then_inc(products_made, 1)

            for step, c, k in SCHEDULE:
                ln = 2 * c + k
                if step == "query":
                    pe.wait_ge(q_ready, c + 1)
                    if c == 0:
                        pe.wait_ge(consts_ready, 7)
                    if c > 0:
                        pe.wait_ge(at_lo_copied, c)
                        pe.wait_ge(at_hi_copied, c)
                        pe.wait_ge(z_lo_copied, 2 * c)
                        pe.wait_ge(z_hi_copied, 2 * c)
                    for hd in range(NH):
                        pe.matmul(bRT[:, G * hd:G * (hd + 1)], MT[:, hd, :], qm[:, c % 2, :], start=True, stop=True)
                    pe.matmul(bZ[1][:, 0:G], Bk[:].rearrange("p n f h -> p (n f h)"), qm[:, c % 2, :],
                              start=True, stop=True).then_inc(r_ready, 1)
                elif step == "scores":
                    if k == 0:
                        pe.wait_ge(r_copied, 4 * (c + 1))
                        if c > 1:
                            pe.wait_ge(shifted, c - 1)
                    q, s = k // 2, k % 2
                    if s == 0:
                        pe.wait_ge(x_ch_in[c][q], 16)
                    for slot in range(2):
                        for j in range(4):
                            g = 16 * q + 4 * j + 2 * slot + s
                            mm = pe.matmul(bS[c % 2][COLT * j:COLT * (j + 1), PIX * k:PIX * (k + 1)],
                                           R[:, c % 2, g, :], xch[:, c % 3, PIX * g:PIX * (g + 1)],
                                           start=(k == 0 and slot == 0), stop=(slot == 1),
                                           skip_group_check=True, tile_position=(0, COLT * j))
                    if k == 7:
                        mm.then_inc(scores_ready, 1)
                elif step == "turn":
                    pe.wait_ge(attn_ready, c + 1)
                    pe.wait_ge(mid_in, 16)
                    for q in range(4):
                        mm = pe.transpose(bRT[:, P * q:P * (q + 1)],
                                          E[:, 2 * q:2 * q + 2, :].rearrange("p s n -> p (s n)"), m("ident"))
                    mm.then_inc(attnT_ready, 1)
                elif step == "z":
                    if k == 0:
                        pe.wait_ge(at_lo_copied, c + 1)
                        pe.wait_ge(at_hi_copied, c + 1)
                        if c > 0:
                            pe.wait_ge(h_ready, c)
                    if k == 2:
                        pe.wait_ge(ck_masked, c + 1)
                    if k % 2 == 0:
                        pe.wait_ge(x_px_in[c][k // 2], 16)
                    for i in range(SLICE):
                        gp = SLICE * k + i
                        at = 4 * NH * (gp % 16)
                        mm = pe.matmul(bZ[k // 2][:, at:at + 4 * NH], xpx[:, c % 2, gp, :],
                                       AT[:, gp].rearrange("p f s h -> p (f s h)"), start=True, stop=True)
                    if k % 2:
                        mm.then_inc(z_ready, 1)
                elif step == "tokens":
                    if c == 0:
                        pe.wait_ge(ao_ready, 2)
                    pe.wait_ge(z_lo_copied, 2 * (c + 1))
                    pe.wait_ge(z_hi_copied, 2 * (c + 1))
                    for hd in range(NH):
                        mm = pe.matmul(bZ[0][:, 0:G], AO[:, hd, :], Z[:, hd].rearrange("p g s -> p (g s)"),
                                       start=(hd == 0), stop=(hd == NH - 1))
                    mm.then_inc(tok_ready, 1)
                elif step == "ln_center":
                    if k == 0:
                        pe.wait_ge(h_ready, c + 1)
                        pe.wait_ge(txt_in[c], 16)
                        if c > 0:
                            pe.wait_ge(hid_relued, 3 * c - 1)
                        src = h[:, c, :]
                    else:
                        pe.wait_ge(h2_ready, c + 1)
                        pe.wait_ge(pt0_copied, c + 1)
                        src = h2[:, c % 2, :]
                    pe.matmul(b5[:, 0:T], m("center"), src, start=True, stop=True).then_inc(xc_ready, 1)
                elif step == "ln_var":
                    pe.wait_ge(sq_ready, ln + 1)
                    if k == 0 and c > 0:
                        pe.wait_ge(hid_relued, 3 * c)
                    if k == 1:
                        pe.wait_ge(pt1_copied, c + 1)
                    pe.matmul(b6[:, 0:T], m("mean"), sq[:], start=True, stop=True).then_inc(var_ready, 1)
                elif step == "qkv":
                    pe.wait_ge(xn_ready, ln + 1)
                    if c > 0:
                        pe.wait_ge(out_ready, c)
                    pe.matmul(b6[:, 0:T], m("wqT"), xn[:], start=True, stop=True)
                    pe.matmul(b7[:, 0:T], m("wkT"), xn[:], start=True, stop=True).then_inc(qk_ready, 1)
                    for a in range(2):
                        mm = pe.matmul(b5[0:TT, P * a:P * (a + 1)], xn[:, TT * a:TT * (a + 1)], m("wvT"),
                                       start=True, stop=True)
                    mm.then_inc(v_ready, 1)
                elif step == "attn_scores":
                    pe.wait_ge(q_copied, c + 1)
                    pe.wait_ge(k_copied, c + 1)
                    for f in range(2):
                        for s in range(2):
                            mm = pe.matmul([b6, b7][f][0:TT, s * T:(s + 1) * T], QT[HALF[f], TT * s:TT * (s + 1)],
                                           KT[HALF[f], :], start=True, stop=True)
                        mm.then_inc(s_ready, 1)
                elif step == "attn_turn":
                    pe.wait_ge(v_copied, c + 1)
                    for f in range(2):
                        pe.wait_ge(p_ready, 4 * c + 2 * f + 2)
                        for s in range(2):
                            for t in range(2):
                                mm = pe.transpose([b5, b6][f][0:TT, T * t + TT * s:T * t + TT * (s + 1)],
                                                  Pr[:, f, s, TT * t:TT * (t + 1)], m("ident")[0:TT, 0:TT])
                        mm.then_inc(pt_ready, 1)
                elif step == "attn_apply":
                    pe.wait_ge(pt0_copied, c + 1)
                    pe.wait_ge(pt1_copied, c + 1)
                    for f in range(2):
                        for t in range(2):
                            mm = pe.matmul(b7[HALF[f], 0:T], V[:, t, D * f:D * (f + 1)], PT[:, f, t, :],
                                           start=(t == 0), stop=(t == 1))
                    mm.then_inc(pv_ready, 1)
                elif step == "expand":
                    pe.wait_ge(xn_ready, 2 * c + 2)
                    for f in range(2):
                        mm = pe.matmul(b7[:, T * f:T * (f + 1)], wiT[:, f, :], xn[:], start=True, stop=True)
                    mm.then_inc(hid_ready, 1)
                elif step == "experts":
                    pe.wait_ge(hid_relued, 3 * c + 1 + k)
                    acc = [b5, b6][k]
                    if k == 0:
                        pe.wait_ge(mid_consts_ready, 1)
                        pe.wait_ge(group_selected, NL * GC * (c + 1))
                    for g in range(GC):
                        pe.matmul(acc[:, RG * g:RG * (g + 1)], sel[:, c % 2, g, k, :],
                                  hid[:, k, RG * g:RG * (g + 1)], start=(g == 0), stop=False,
                                  skip_group_check=True)
                    mm = pe.matmul(acc[:, 0:2 * T], brs[:, k, :],
                                   onehot[:, GC * c:GC * (c + 1)].rearrange("p (g o) -> p g o", o=1)
                                   .to_broadcast([P, GC, RG]), start=False, stop=True, skip_group_check=True)
                    mm.then_inc(hid_ready, 1)
                elif step == "project":
                    pe.wait_ge(hid_relued, 3 * c + 3)
                    for f in range(2):
                        mm = pe.matmul(b7[HALF[f], 0:T], m("woT"), hid[:, NL, T * f:T * (f + 1)], start=True, stop=True)
                    mm.then_inc(wo_ready, 1)


def kernel(**inputs):
    import numpy as np
    import concourse.bacc as bacc
    from concourse.bass_utils import run_bass_kernel_spmd

    a = {k: np.asarray(v) for k, v in inputs.items()}
    f32 = np.float32
    x = a["x"].reshape(C, 2, D, 8, 8, 8, 8)
    x = x.transpose(0, 1, 2, 3, 5, 4, 6).reshape(C, P, G, PIX)
    x_ch = np.ascontiguousarray(x.reshape(C, P, G * PIX))
    x_px = np.ascontiguousarray(
        x.reshape(C, P, G // 2, 2, PIX).transpose(0, 3, 4, 2, 1).reshape(C, P, G // 2, P))
    txt = np.ascontiguousarray(a["txt"].reshape(C, 2, TXT, D).transpose(0, 1, 3, 2).reshape(C, P, TXT))

    def twice(v):
        return np.concatenate([v, v], axis=0)

    def put(dst, at, v):
        dst[:v.shape[0], at[0]:at[0] + v.shape[1]] = v

    def diag2(v):
        out = np.zeros((P, P), f32)
        out[:D, :D] = v
        out[D:, D:] = v
        return out

    w8 = np.zeros((DH, W8_N), f32)
    for name, key in (("wq", "L0_tok_Wq"), ("wk", "L0_tok_Wk"), ("wv", "L0_tok_Wv")):
        v = a[key].reshape(NH, DH, D).transpose(1, 0, 2)
        put(w8, W8[name], np.concatenate([v, v], axis=2).reshape(DH, NH * P))
    put(w8, W8["wo"], a["L0_tok_Wo"].reshape(D, NH, DH).transpose(2, 1, 0).reshape(DH, NH * D))
    put(w8, W8["bq"], a["L0_tok_bq"].reshape(NH, DH).T)
    put(w8, W8["bk"], a["L0_tok_bk"].reshape(NH, DH).T)

    early = np.zeros((P, EARLY_N), f32)
    put(early, EARLY["woT"], np.concatenate([a["L0_tok_Wo"].T] * 2, axis=1))
    put(early, EARLY["bv"], a["L0_tok_bv"][:, None])
    put(early, EARLY["bo"], twice(a["L0_tok_bo"])[:, None])
    put(early, EARLY["bqr"], np.concatenate([a["L0_tok_bq"].reshape(NH, DH)] * 16))
    put(early, EARLY["bkr"], np.concatenate([a["L0_tok_bk"].reshape(NH, DH)] * 16))
    put(early, EARLY["mask"], np.repeat(np.eye(NH, dtype=f32), SLOT, axis=0))

    mid = np.zeros((P, MID_N), f32)
    put(mid, MID["ident"], np.eye(P, dtype=f32))
    put(mid, MID["center"], diag2(np.eye(D, dtype=f32) - f32(1.0 / D)))
    put(mid, MID["mean"], diag2(np.full((D, D), 1.0 / D, f32)))
    put(mid, MID["wqT"], diag2(a["L0_attn_Wq"].T))
    put(mid, MID["wkT"], diag2(a["L0_attn_Wk"].T))
    put(mid, MID["wvT"], diag2(a["L0_attn_Wv"].T))
    put(mid, MID["bq"], twice(a["L0_attn_bq"])[:, None])
    put(mid, MID["bk"], twice(a["L0_attn_bk"])[:, None])
    put(mid, MID["bv"], twice(a["L0_attn_bv"])[:, None])
    wi = np.zeros((P, 2, P), f32)
    wi[:D, 0] = a["L0_ffn_Wi"].T
    wi[D:, 1] = a["L0_ffn_Wi"].T
    put(mid, MID["wiT"], wi.reshape(P, 2 * P))
    put(mid, MID["bi"], a["L0_ffn_bi"][:, None])
    put(mid, MID["woT"], a["L0_ffn_Wo"].T)
    put(mid, MID["bo"], twice(a["L0_ffn_bo"])[:, None])
    br = np.zeros((P, NL, HID), f32)
    br[:NE] = a["L0_ffn_br"].transpose(1, 0, 2)
    br[NE] = a["L0_ffn_bs"][:, 0]
    put(mid, MID["brs"], br.reshape(P, NL * HID))
    rows = np.arange(P)
    put(mid, MID["expert"], np.where(rows < NE, rows, -1).astype(f32)[:, None])
    put(mid, MID["shared"], (rows == NE).astype(f32)[:, None])
    put(mid, MID["beta"], np.broadcast_to(a["L0_attn_beta"], (P, 2)))
    idx = np.arange(T, dtype=f32)
    dist = np.abs(idx[:, None] - idx[None, :])
    cosines = [np.cos(f32(2.0 * np.pi) * dist / f32(t)).astype(f32) for t in (24.0, 720.0)]
    cosines = np.stack(cosines).reshape(2, 2, TT, T).transpose(2, 0, 1, 3)
    put(mid, MID["cos"], cosines.reshape(TT, 2 * 2 * T))
    put(mid, MID["wsT"], a["L0_ffn_Ws"][:, 0].transpose(2, 0, 1).reshape(P, NL * HID))

    arrays = {
        "x_ch": x_ch, "x_px": x_px, "txt_ch": txt, "w8_in_dram": w8, "early_in_dram": early, "mid_in_dram": mid,
        "wrT_in": np.ascontiguousarray(a["L0_ffn_Wr"].transpose(3, 0, 1, 2)),
        "route_ids": np.ascontiguousarray(np.broadcast_to(a["L0_ffn_route_id"], (P, 64))),
    }
    nc = bacc.Bacc("TRN2", target_bir_lowering=False, num_devices=1)
    args = [nc.dram_tensor(n, v.shape, mybir.dt.from_np(v.dtype), kind="ExternalInput").ap() for n, v in arrays.items()]
    args.append(nc.dram_tensor("out_dram", (C, P, T), F32, kind="ExternalOutput").ap())
    early_fusion_kernel(nc, *args)
    r = run_bass_kernel_spmd(nc, [arrays], core_ids=[0])
    got = r.results[0]["out_dram"].reshape(C, 2, D, T).transpose(0, 1, 3, 2)
    return np.ascontiguousarray(got.reshape(B, T, D))
```

```python
from contextlib import ExitStack

import concourse.bass as bass
from concourse import mybir

F32 = mybir.dt.float32
I32 = mybir.dt.int32
ALU = mybir.AluOpType
ACT = mybir.ActivationFunctionType
AX = mybir.AxisListType.X

P = 128
D = 64
NH, DH = 8, 8
B = 8
C = B // 2
G = 64
PIX = 64
QUART = 16
SLICE = 8
SLOT = 2 * NH
COLT = 32
TXT = 128
T = G + TXT
TT = T // 2
HID = 128
NE = 16
NL = 2
RG = B * T // 64
GC = 2 * T // RG
LN_EPS = 1e-5



def _columns(parts):
    at, out = 0, {}
    for name, n in parts:
        out[name] = (at, n)
        at += n
    return out, at


EARLY, EARLY_N = _columns([("wqT", P), ("wk", P), ("bk", P), ("bq", 1), ("bv", 1), ("bo", 1), ("head", NH), ("mask", NH)])
MID, MID_N = _columns([
    ("ident", P), ("tvT", P), ("toT", P), ("center", P), ("mean", P), ("wqT", P), ("wkT", P), ("wvT", P), ("bq", 1),
    ("bk", 1), ("bv", 1), ("wiT", 2 * P), ("bi", 1), ("woT", D), ("bo", 1), ("brs", NL * HID), ("expert", 1),
    ("shared", 1), ("beta", 2), ("cos", 2 * 2 * T), ("wsT", NL * HID)])


def early_fusion_kernel(nc: bass.Bass, x_ch, x_px, txt, early_d, mid_d, wrT_d, route_d, out):
    with ExitStack() as ctx:
        def sb(name, shape, dt=F32):
            return ctx.enter_context(nc.sbuf_tensor(name, shape, dt))

        def sem(name):
            return ctx.enter_context(nc.semaphore(name))

        xch = sb("xch", [P, 3, G * PIX])
        xpx = sb("xpx", [P, 2, G // 2, P])
        early = sb("early", [P, EARLY_N])
        mid = sb("mid", [P, MID_N])
        wrT = sb("wrT", [P, NL, NE, HID])
        sel = sb("sel", [P, 2, GC, NL, HID])
        wsI = sb("wsI", [P, NL, HID])
        route = sb("route", [P, 64], I32)
        onehot = sb("onehot", [P, 64])
        biasg = sb("biasg", [P, NL, 64])
        epsc = sb("epsc", [P, 1])
        cosb = sb("cosb", [P, 2, T])
        qsum = sb("qsum", [P, 2, G])
        qm = sb("qm", [P, 2, G])
        qp = sb("qp", [P, G])
        qph = sb("qph", [P, G, NH])
        R = sb("R", [P, 2, G, COLT])
        ck = sb("ck", [P, G])
        cc = sb("cc", [P, 8])
        mx = sb("mx", [P, 8])
        sh = sb("sh", [P, 8])
        nsh = sb("nsh", [P, 8])
        E = sb("E", [P, 8, PIX])
        den = sb("den", [P, 8])
        rden = sb("rden", [P, 8])
        AT = sb("AT", [P, G // 2, 2, COLT])
        zc = sb("zc", [P, 4, P])
        Z = sb("Z", [P, G, NH])
        ctm = sb("ctm", [P, G, NH])
        ctx_sum = sb("ctx_sum", [P, G])
        ctxv = sb("ctxv", [P, G])
        h = sb("h", [P, C, T])
        h2 = sb("h2", [P, 2, T])
        sq = sb("sq", [P, T])
        lv = sb("lv", [P, T])
        rstd = sb("rstd", [P, T])
        xn = sb("xn", [P, T])
        QT = sb("QT", [P, T])
        KT = sb("KT", [P, T])
        V = sb("V", [TT, 2, P])
        Pr = sb("Pr", [TT, 2, 2, T])
        nmx = sb("nmx", [TT, 4])
        pden = sb("pden", [TT, 4])
        prden = sb("prden", [TT, 4])
        PT = sb("PT", [TT, 2, 2, T])
        hid = sb("hid", [P, NL + 1, 2 * T + COLT - RG])
        yt = sb("yt", [P, 4, HID])
        hpre = sb("hpre", [P, GC, RG])
        outT = sb("outT", [P, C, T])

        bank = [ctx.enter_context(nc.psum_tensor(f"bank{i}", [P, 512], F32)) for i in range(8)]
        bS = [bank[0], bank[1]]
        bRT = bank[2]
        bZ, bW = bank[3], bank[4]
        b5, b6, b7 = bank[5], bank[6], bank[7]

        x_ch_in = [[sem(f"x_ch_in{c}_{k}") for k in range(4)] for c in range(C)]
        x_px_in = [[sem(f"x_px_in{c}_{k}") for k in range(2)] for c in range(C)]
        txt_in = [sem(f"txt_in{c}") for c in range(C)]
        early_in, mid_in, wr_in, route_in = (sem(n) for n in ("early_in", "mid_in", "wr_in", "route_in"))
        out_stored = [sem(f"out_stored{c}") for c in range(C)]
        dve_zeroed, pool_zeroed, onehot_ready, bias_part, cosb_ready, biasg_made, biasg_ready = (
            sem(n) for n in ("dve_zeroed", "pool_zeroed", "onehot_ready", "bias_part", "cosb_ready", "biasg_made", "biasg_ready"))
        wsi_ready, group_selected = (sem(n) for n in ("wsi_ready", "group_selected"))
        qsum_ready, q_ready, qp_made, qp_ready, qph_ready, c_made, r_ready, r_lo_copied, r_hi_copied, ck_masked, cc_ready = (
            sem(n) for n in ("qsum_ready", "q_ready", "qp_made", "qp_ready", "qph_ready", "c_made", "r_ready",
                             "r_lo_copied", "r_hi_copied", "ck_masked", "cc_ready"))
        scores_ready, mx_ready, sh_ready, nsh_ready, shifted, exp_ready = (
            sem(n) for n in ("scores_ready", "mx_ready", "sh_ready", "nsh_ready", "shifted", "exp_ready"))
        den_ready, rden_ready, attn_ready, attnT_ready, at_lo_copied, at_hi_copied = (
            sem(n) for n in ("den_ready", "rden_ready", "attn_ready", "attnT_ready", "at_lo_copied", "at_hi_copied"))
        z_ready, zc_ready, zt_ready, z_copied, ctx_ready, ctx_masked, ctx_summed, ctxv_ready, tok_ready, h_ready = (
            sem(n) for n in ("z_ready", "zc_ready", "zt_ready", "z_copied", "ctx_ready", "ctx_masked", "ctx_summed",
                             "ctxv_ready", "tok_ready", "h_ready"))
        xc_ready, sq_ready, var_ready, lv_ready, rstd_ready, xn_ready = (
            sem(n) for n in ("xc_ready", "sq_ready", "var_ready", "lv_ready", "rstd_ready", "xn_ready"))
        qk_ready, v_ready, q_copied, k_copied, v_copied, s_ready, biased, pexp_ready = (
            sem(n) for n in ("qk_ready", "v_ready", "q_copied", "k_copied", "v_copied", "s_ready", "biased", "pexp_ready"))
        prden_ready, p_ready, pt_ready, pt0_copied, pt1_copied, pv_ready, h2_ready = (
            sem(n) for n in ("prden_ready", "p_ready", "pt_ready", "pt0_copied", "pt1_copied", "pv_ready", "h2_ready"))
        expand_ready, y_ready, yt_ready, ytt_ready, hpre_ready, hid_relued, wo_ready, out_ready = (
            sem(n) for n in ("expand_ready", "y_ready", "yt_ready", "ytt_ready", "hpre_ready", "hid_relued", "wo_ready", "out_ready"))

        def e(name, rows=slice(0, P)):
            at, n = EARLY[name]
            return early[rows, at:at + n]

        def m(name, rows=slice(0, P)):
            at, n = MID[name]
            return mid[rows, at:at + n]

        HALF = [slice(0, D), slice(D, P)]
        INV = float(DH) ** -0.5
        wiT = m("wiT").rearrange("p (f n) -> p f n", f=2)
        brs = m("brs").rearrange("p (l n) -> p l n", l=NL)
        wsT = m("wsT").rearrange("p (l n) -> p l n", l=NL)
        cos = m("cos").rearrange("p (n a t) -> p n a t", n=2, a=2)

        def interval(c):
            a, b, p = c, c + 1, c + 2
            order = [
                ("scores", b, 0), ("ln_center", a, 0), ("pool", p, 0), ("scores", b, 1), ("ln_var", a, 0),
                ("scores", b, 2), ("scores", b, 3), ("pool", p, 1), ("qkv", a, 0), ("scores", b, 4), ("scores", b, 5),
                ("attn_scores", a, 0), ("scores", b, 6), ("scores", b, 7), ("shift", b, 0), ("setup", b, 0),
                ("attn_norm", a, 0), ("attn_turn", a, 0), ("normalise", b, 0), ("attn_apply", a, 0),
                ("turn", b, 0), ("ln_center", a, 1), ("z", b, 0), ("ln_var", a, 1), ("z", b, 1),
                ("z", b, 2), ("expand", a, 0), ("z", b, 3), ("pool", p, 2), ("experts", a, 0), ("zturn", b, 0),
                ("experts_turn", a, 0), ("context", b, 0), ("experts", a, 1), ("pool", p, 3), ("tokens", b, 0),
                ("experts_turn", a, 1), ("query", p, 0), ("project", a, 0)]
            return [s for s in order if 0 <= s[1] < C and (s[0] != "setup" or s[1] == 0)]

        SCHEDULE = [("pool", 0, k) for k in range(4)] + [("query", 0, 0)]
        for c in range(-1, C):
            SCHEDULE += interval(c)

        def r_src(f, slot):
            return bRT[:].rearrange("p (m k s h) -> p m k s h", k=2, s=2, h=NH)[HALF[f], :, slot]

        def r_dst(c, f, slot):
            at = SLOT * slot + NH * f
            return R[:, c % 2].rearrange("p (m k s) n -> p m k s n", k=2, s=2)[HALF[f], :, slot, :, at:at + NH]

        def at_src(sp, slot):
            return bRT[:].rearrange("p (m k f h) -> p m k f h", k=2, f=2, h=NH)[HALF[sp], :, slot]

        def at_dst(sp, slot):
            at = SLOT * slot + NH * sp
            return AT[:].rearrange("p (m k) f n -> p m k f n", k=2)[HALF[sp], :, slot, :, at:at + NH]

        block = ctx.enter_context(nc.Block())

        @block.sync
        def _(sp):
            def load_ch(c):
                if c >= 3:
                    sp.wait_ge(scores_ready, c - 2)
                for k in range(4):
                    cols = slice(k * QUART * PIX, (k + 1) * QUART * PIX)
                    sp.dma_start(xch[:, c % 3, cols], x_ch[c, :, cols]).then_inc(x_ch_in[c][k], 16)

            def load_px(c):
                if c >= 2:
                    sp.wait_ge(z_ready, c - 1)
                for k in range(2):
                    gp = slice(k * G // 4, (k + 1) * G // 4)
                    sp.dma_start(xpx[:, c % 2, gp, :], x_px[c, :, gp, :]).then_inc(x_px_in[c][k], 16)

            load_ch(0)
            sp.dma_start(route[:], route_d).then_inc(route_in, 16)
            load_px(0)
            sp.dma_start(mid[:], mid_d).then_inc(mid_in, 16)
            load_ch(1)
            sp.dma_start(wrT[:], wrT_d).then_inc(wr_in, 16)
            for c in range(C):
                sp.dma_start(h[:, c, G:T], txt[c]).then_inc(txt_in[c], 16)
            load_px(1)
            load_ch(2)
            load_ch(3)
            load_px(2)
            load_px(3)
            for c in range(C):
                sp.wait_ge(out_ready, c + 1)
                sp.dma_start(out[c], outT[:, c, :]).then_inc(out_stored[c], 16)
            for c in range(C):
                sp.wait_ge(out_stored[c], 16)

        @block.gpsimd
        def _(pool):
            pool.memset(AT[:], 0.0).then_inc(pool_zeroed, 1)
            pool.memset(R[:, 1], 0.0).then_inc(pool_zeroed, 1)
            pool.wait_ge(mid_in, 16)
            for l in range(NL):
                pool.tensor_tensor(wsI[:, l, :], wsT[:, l, :], m("ident"), ALU.add).then_inc(wsi_ready, 1)
            pool.wait_ge(wsi_ready, NL)
            pool.wait_ge(wr_in, 16)
            pool.wait_ge(route_in, 16)
            for c in range(C):
                if c >= 2:
                    pool.wait_ge(y_ready, NL * (c - 1))
                with pool.Fori(0, GC) as g:
                    ex = pool.value_load(route[0:1, bass.ds(g + GC * c, 1)], min_val=0, max_val=NE - 1)
                    for l in range(NL):
                        pool.tensor_tensor(sel[:, c % 2, bass.ds(g, 1), l, :], wrT[:, l, bass.ds(ex, 1), :],
                                           wsI[:, l:l + 1, :], ALU.add).then_inc(group_selected, 1)

        @block.scalar
        def _(act):
            act.dma_start(early[:], early_d).then_inc(early_in, 16)

            for step, c, k in SCHEDULE:
                ln = 2 * c + k
                if step == "shift":
                    act.wait_ge(shifted, c + 1)
                    act.activation(E[:], E[:], ACT.Exp).then_inc(exp_ready, 1)
                elif step == "query":
                    act.wait_ge(r_ready, c + 1)
                    if c == 0:
                        act.wait_ge(dve_zeroed, 2)
                    if c == 1:
                        act.wait_ge(pool_zeroed, 1)
                    for slot in range(2):
                        act.activation(r_dst(c, 0, slot), r_src(0, slot), ACT.Copy).then_inc(r_lo_copied, 1)
                elif step == "turn":
                    act.wait_ge(attnT_ready, c + 1)
                    if c == 0:
                        act.wait_ge(pool_zeroed, 2)
                    if c > 0:
                        act.wait_ge(z_ready, c)
                    for slot in range(2):
                        act.activation(at_dst(0, slot), at_src(0, slot), ACT.Copy).then_inc(at_lo_copied, 1)
                elif step == "z" and k == 3:
                    act.wait_ge(z_ready, c + 1)
                    if c > 0:
                        act.wait_ge(zt_ready, c)
                    act.activation(zc[:], bZ[:].rearrange("p (q n) -> p q n", q=4), ACT.Copy).then_inc(zc_ready, 1)
                elif step == "zturn":
                    act.wait_ge(zt_ready, c + 1)
                    if c > 0:
                        act.wait_ge(ctx_ready, c)
                    act.activation(Z[:], bW[:].rearrange("p (g h) -> p g h", h=NH), ACT.Copy).then_inc(z_copied, 1)
                elif step == "ln_center":
                    act.wait_ge(xc_ready, ln + 1)
                    act.activation(sq[:], b5[:, 0:T], ACT.Square).then_inc(sq_ready, 1)
                elif step == "ln_var":
                    act.wait_ge(var_ready, ln + 1)
                    if ln == 0:
                        act.wait_ge(dve_zeroed, 1)
                    act.activation(lv[:], b6[:, 0:T], ACT.Ln, bias=epsc[:, 0:1]).then_inc(lv_ready, 1)
                    act.wait_ge(lv_ready, ln + 1)
                    if ln > 0:
                        act.wait_ge(xn_ready, ln)
                    act.activation(rstd[:], lv[:], ACT.Exp, scale=-0.5).then_inc(rstd_ready, 1)
                elif step == "qkv":
                    act.wait_ge(qk_ready, c + 1)
                    act.activation(KT[:], b7[:, 0:T], ACT.Identity, bias=m("bk")).then_inc(k_copied, 1)
                    act.wait_ge(v_ready, c + 1)
                    act.activation(V[:], b5[0:TT, 0:2 * P].rearrange("p (a n) -> p a n", a=2),
                                   ACT.Copy).then_inc(v_copied, 1)
                elif step == "attn_scores":
                    for i in range(4):
                        act.wait_ge(biased, 4 * c + i + 1)
                        act.activation(Pr[:, i // 2, i % 2, :], Pr[:, i // 2, i % 2, :], ACT.Exp,
                                       bias=nmx[:, i:i + 1], scale=-1.0,
                                       accum_out=pden[:, i:i + 1]).then_inc(pexp_ready, 1)
                elif step == "attn_turn":
                    act.wait_ge(pt_ready, 2 * c + 1)
                    act.activation(PT[:, 0], b5[0:TT, 0:2 * T].rearrange("p (a t) -> p a t", a=2),
                                   ACT.Copy).then_inc(pt0_copied, 1)
                elif step == "expand":
                    act.wait_ge(expand_ready, c + 1)
                    act.activation(hid[:, 0, 0:2 * T], b7[:, 0:2 * T], ACT.Relu, bias=m("bi")).then_inc(hid_relued, 1)
                elif step == "experts":
                    act.wait_ge(y_ready, NL * c + k + 1)
                    if c + k > 0:
                        act.wait_ge(ytt_ready, NL * c + k)
                    act.activation(yt[:], b5[:].rearrange("p (b n) -> p b n", b=4), ACT.Copy).then_inc(yt_ready, 1)
                elif step == "experts_turn":
                    act.wait_ge(hpre_ready, NL * c + k + 1)
                    act.activation(hid[:, k + 1, 0:2 * T], hpre[:].rearrange("p g n -> p (g n)"),
                                   ACT.Relu).then_inc(hid_relued, 1)

        @block.vector
        def _(dve):
            dve.memset(epsc[:], LN_EPS).then_inc(dve_zeroed, 1)
            dve.memset(R[:, 0], 0.0).then_inc(dve_zeroed, 1)
            dve.memset(hid[:, :, 2 * T:], 0.0).then_inc(dve_zeroed, 1)

            for step, c, k in SCHEDULE:
                ln = 2 * c + k
                if step == "pool":
                    dve.wait_ge(x_ch_in[c][k], 16)
                    dve.tensor_reduce(qsum[:, c % 2, QUART * k:QUART * (k + 1)],
                                      xch[:, c % 3, QUART * PIX * k:QUART * PIX * (k + 1)]
                                      .rearrange("p (g n) -> p g n", n=PIX), AX, ALU.add).then_inc(qsum_ready, 1)
                elif step == "query":
                    dve.wait_ge(qsum_ready, 4 * (c + 1))
                    dve.tensor_scalar(qm[:, c % 2, :], qsum[:, c % 2, :], 1.0 / PIX, None, ALU.mult).then_inc(q_ready, 1)
                    if c == 0:
                        dve.wait_ge(early_in, 16)
                    dve.wait_ge(qp_made, c + 1)
                    dve.tensor_scalar(qp[:], bW[:, 0:G], e("bq"), INV, ALU.add, ALU.mult).then_inc(qp_ready, 1)
                    dve.wait_ge(qp_ready, c + 1)
                    dve.tensor_tensor(qph[:], qp[:].rearrange("p (g o) -> p g o", o=1).to_broadcast([P, G, NH]),
                                      e("head").rearrange("p (o h) -> p o h", o=1).to_broadcast([P, G, NH]),
                                      ALU.mult).then_inc(qph_ready, 1)
                    dve.wait_ge(c_made, c + 1)
                    dve.tensor_tensor(ck[:].rearrange("p (q n s) -> p q n s", q=4, s=2),
                                      bW[:, G:2 * G].rearrange("p (q n s) -> p q n s", q=4, s=2),
                                      e("mask").rearrange("p (o n q) -> p o n q", o=1, q=1).to_broadcast([P, 4, NH, 2]),
                                      ALU.mult).then_inc(ck_masked, 1)
                    dve.wait_ge(ck_masked, c + 1)
                    dve.tensor_reduce(cc[:].rearrange("p (q s) -> p q s", s=2),
                                      ck[:].rearrange("p (q n s) -> p q s n", q=4, s=2), AX, ALU.add).then_inc(cc_ready, 1)
                    dve.wait_ge(r_ready, c + 1)
                    if c == 0:
                        dve.wait_ge(dve_zeroed, 2)
                    if c == 1:
                        dve.wait_ge(pool_zeroed, 1)
                    for slot in range(2):
                        dve.tensor_copy(r_dst(c, 1, slot), r_src(1, slot)).then_inc(r_hi_copied, 1)
                elif step == "setup":
                    dve.wait_ge(mid_in, 16)
                    dve.wait_ge(route_in, 16)
                    dve.tensor_scalar(onehot[:], route[:], m("expert"), m("shared"), ALU.is_equal,
                                      ALU.add).then_inc(onehot_ready, 1)
                    dve.tensor_scalar(cosb[0:TT], cos[0:TT, 0], m("beta")[0:TT, 0:1], None, ALU.mult).then_inc(bias_part, 1)
                    dve.wait_ge(bias_part, 1)
                    dve.scalar_tensor_tensor(out=cosb[0:TT], in0=cos[0:TT, 1], scalar=m("beta")[0:TT, 1:2], in1=cosb[0:TT],
                                             op0=ALU.mult, op1=ALU.add).then_inc(cosb_ready, 1)
                    dve.wait_ge(biasg_made, 1)
                    dve.tensor_copy(biasg[:], b5[:, 0:NL * 64].rearrange("p (l g) -> p l g", l=NL)).then_inc(biasg_ready, 1)
                elif step == "shift":
                    S = bS[c % 2][:].rearrange("p (s n) -> p s n", n=PIX)
                    dve.wait_ge(scores_ready, c + 1)
                    dve.tensor_reduce(mx[:], S, AX, ALU.max).then_inc(mx_ready, 1)
                    dve.wait_ge(mx_ready, c + 1)
                    dve.wait_ge(cc_ready, c + 1)
                    dve.tensor_tensor(sh[:], mx[:], cc[:], ALU.add).then_inc(sh_ready, 1)
                    dve.wait_ge(sh_ready, c + 1)
                    dve.tensor_tensor(nsh[:], cc[:], sh[:], ALU.subtract).then_inc(nsh_ready, 1)
                    dve.wait_ge(nsh_ready, c + 1)
                    if c > 0:
                        dve.wait_ge(attnT_ready, c)
                    dve.tensor_tensor(E[:], S, nsh[:].rearrange("p (s o) -> p s o", o=1).to_broadcast([P, 8, PIX]),
                                      ALU.add).then_inc(shifted, 1)
                elif step == "normalise":
                    dve.wait_ge(exp_ready, c + 1)
                    dve.tensor_reduce(den[:], E[:], AX, ALU.add).then_inc(den_ready, 1)
                    dve.wait_ge(den_ready, c + 1)
                    dve.reciprocal(rden[:], den[:]).then_inc(rden_ready, 1)
                    dve.wait_ge(rden_ready, c + 1)
                    dve.tensor_tensor(E[:], E[:], rden[:].rearrange("p (s o) -> p s o", o=1).to_broadcast([P, 8, PIX]),
                                      ALU.mult).then_inc(attn_ready, 1)
                elif step == "turn":
                    dve.wait_ge(attnT_ready, c + 1)
                    if c == 0:
                        dve.wait_ge(pool_zeroed, 2)
                    if c > 0:
                        dve.wait_ge(z_ready, c)
                    for slot in range(2):
                        dve.tensor_copy(at_dst(1, slot), at_src(1, slot)).then_inc(at_hi_copied, 1)
                elif step == "context":
                    dve.wait_ge(ctx_ready, c + 1)
                    dve.tensor_tensor(ctm[:], bZ[:].rearrange("p (g h) -> p g h", h=NH),
                                      e("head").rearrange("p (o h) -> p o h", o=1).to_broadcast([P, G, NH]),
                                      ALU.mult).then_inc(ctx_masked, 1)
                    dve.wait_ge(ctx_masked, c + 1)
                    dve.tensor_reduce(ctx_sum[:], ctm[:], AX, ALU.add).then_inc(ctx_summed, 1)
                    dve.wait_ge(ctx_summed, c + 1)
                    dve.tensor_scalar(ctxv[:], ctx_sum[:], e("bv"), None, ALU.add).then_inc(ctxv_ready, 1)
                elif step == "tokens":
                    dve.wait_ge(tok_ready, c + 1)
                    dve.scalar_tensor_tensor(out=h[:, c, 0:G], in0=bW[:, 0:G], scalar=e("bo"), in1=qm[:, c % 2, :],
                                             op0=ALU.add, op1=ALU.add).then_inc(h_ready, 1)
                elif step == "ln_var":
                    dve.wait_ge(rstd_ready, ln + 1)
                    dve.tensor_tensor(xn[:], b5[:, 0:T], rstd[:], ALU.mult).then_inc(xn_ready, 1)
                elif step == "qkv":
                    dve.wait_ge(qk_ready, c + 1)
                    dve.tensor_scalar(QT[:], b6[:, 0:T], m("bq"), float(D) ** -0.5, ALU.add, ALU.mult).then_inc(q_copied, 1)
                elif step == "attn_scores":
                    for i in range(4):
                        f, s = i // 2, i % 2
                        dve.wait_ge(s_ready, 2 * c + f + 1)
                        if i == 0 and c == 0:
                            dve.wait_ge(cosb_ready, 1)
                        dve.tensor_tensor_reduce(Pr[:, f, s, :], [b6, b7][f][0:TT, s * T:(s + 1) * T], cosb[0:TT, s, :],
                                                 -1.0, 3.0e38, ALU.add, ALU.min, nmx[:, i:i + 1]).then_inc(biased, 1)
                elif step == "attn_norm":
                    dve.wait_ge(pexp_ready, 4 * (c + 1))
                    dve.reciprocal(prden[:], pden[:]).then_inc(prden_ready, 1)
                    dve.wait_ge(prden_ready, c + 1)
                    for i in range(4):
                        dve.tensor_scalar(Pr[:, i // 2, i % 2, :], Pr[:, i // 2, i % 2, :], prden[:, i:i + 1], None,
                                          ALU.mult).then_inc(p_ready, 1)
                elif step == "attn_turn":
                    dve.wait_ge(pt_ready, 2 * c + 2)
                    dve.tensor_copy(PT[:, 1], b6[0:TT, 0:2 * T].rearrange("p (a t) -> p a t", a=2)).then_inc(pt1_copied, 1)
                elif step == "attn_apply":
                    dve.wait_ge(pv_ready, c + 1)
                    dve.scalar_tensor_tensor(out=h2[:, c % 2, :], in0=b7[:, 0:T], scalar=m("bv"), in1=h[:, c, :],
                                             op0=ALU.add, op1=ALU.add).then_inc(h2_ready, 1)
                elif step == "experts_turn":
                    dve.wait_ge(ytt_ready, NL * c + k + 1)
                    if c + k > 0:
                        dve.wait_ge(hid_relued, 3 * c + 2 * k)
                    if c + k == 0:
                        dve.wait_ge(biasg_ready, 1)
                    dve.tensor_tensor(hpre[:], b6[:].rearrange("p (g n) -> p g n", n=COLT)[:, :, 0:RG],
                                      biasg[:, k, GC * c:GC * (c + 1)].rearrange("p (g o) -> p g o", o=1)
                                      .to_broadcast([P, GC, RG]), ALU.add).then_inc(hpre_ready, 1)
                elif step == "project":
                    dve.wait_ge(wo_ready, c + 1)
                    dve.scalar_tensor_tensor(out=outT[:, c, :], in0=b7[:, 0:T], scalar=m("bo"), in1=h2[:, c % 2, :],
                                             op0=ALU.add, op1=ALU.add).then_inc(out_ready, 1)

        @block.tensor
        def _(pe):
            for step, c, k in SCHEDULE:
                ln = 2 * c + k
                if step == "query":
                    pe.wait_ge(q_ready, c + 1)
                    if c == 0:
                        pe.wait_ge(early_in, 16)
                    if c > 0:
                        pe.wait_ge(h_ready, c)
                        pe.wait_ge(at_lo_copied, 2 * c)
                        pe.wait_ge(at_hi_copied, 2 * c)
                    pe.matmul(bW[:, 0:G], e("wqT"), qm[:, c % 2, :], start=True, stop=True).then_inc(qp_made, 1)
                    pe.wait_ge(qp_ready, c + 1)
                    pe.matmul(bW[:, G:2 * G], e("bk"), qp[:], start=True, stop=True).then_inc(c_made, 1)
                    pe.wait_ge(qph_ready, c + 1)
                    pe.matmul(bRT[:], e("wk"), qph[:].rearrange("p g h -> p (g h)"), start=True, stop=True).then_inc(r_ready, 1)
                elif step == "scores":
                    if k == 0:
                        pe.wait_ge(r_lo_copied, 2 * (c + 1))
                        pe.wait_ge(r_hi_copied, 2 * (c + 1))
                        if c > 1:
                            pe.wait_ge(shifted, c - 1)
                    q, s = k // 2, k % 2
                    if s == 0:
                        pe.wait_ge(x_ch_in[c][q], 16)
                    for slot in range(2):
                        for j in range(4):
                            g = 16 * q + 4 * j + 2 * slot + s
                            mm = pe.matmul(bS[c % 2][COLT * j:COLT * (j + 1), PIX * k:PIX * (k + 1)],
                                           R[:, c % 2, g, :], xch[:, c % 3, PIX * g:PIX * (g + 1)],
                                           start=(k == 0 and slot == 0), stop=(slot == 1),
                                           skip_group_check=True, tile_position=(0, COLT * j))
                    if k == 7:
                        mm.then_inc(scores_ready, 1)
                elif step == "turn":
                    pe.wait_ge(attn_ready, c + 1)
                    pe.wait_ge(mid_in, 16)
                    for q in range(4):
                        mm = pe.transpose(bRT[:, P * q:P * (q + 1)],
                                          E[:, 2 * q:2 * q + 2, :].rearrange("p s n -> p (s n)"), m("ident"))
                    mm.then_inc(attnT_ready, 1)
                elif step == "z":
                    if k == 0:
                        pe.wait_ge(at_lo_copied, 2 * (c + 1))
                        pe.wait_ge(at_hi_copied, 2 * (c + 1))
                        if c > 0:
                            pe.wait_ge(ctx_masked, c)
                    if k % 2 == 0:
                        pe.wait_ge(x_px_in[c][k // 2], 16)
                    for f in range(2):
                        for slot in range(2):
                            for j in range(4):
                                gp = 8 * k + 2 * j + slot
                                mm = pe.matmul(bZ[COLT * j:COLT * (j + 1), P * k + D * f:P * k + D * (f + 1)],
                                               AT[:, gp, f, :], xpx[:, c % 2, gp, D * f:D * (f + 1)],
                                               start=(k == 0 and f == 0 and slot == 0), stop=(slot == 1),
                                               skip_group_check=True, tile_position=(0, COLT * j))
                    if k == 3:
                        mm.then_inc(z_ready, 1)
                elif step == "zturn":
                    pe.wait_ge(zc_ready, c + 1)
                    pe.wait_ge(cc_ready, c + 1)
                    for q in range(4):
                        mm = pe.transpose(bW[:, P * q:P * (q + 1)], zc[:, q, :], m("ident"))
                    mm.then_inc(zt_ready, 1)
                elif step == "context":
                    pe.wait_ge(z_copied, c + 1)
                    pe.matmul(bZ[:], m("tvT"), Z[:].rearrange("p g h -> p (g h)"), start=True, stop=True).then_inc(ctx_ready, 1)
                elif step == "tokens":
                    pe.wait_ge(ctxv_ready, c + 1)
                    pe.matmul(bW[:, 0:G], m("toT"), ctxv[:], start=True, stop=True).then_inc(tok_ready, 1)
                elif step == "setup":
                    pe.wait_ge(onehot_ready, 1)
                    for l in range(NL):
                        mm = pe.matmul(b5[:, 64 * l:64 * (l + 1)], brs[:, l, :], onehot[:], start=True, stop=True)
                    mm.then_inc(biasg_made, 1)
                elif step == "ln_center":
                    if k == 0:
                        pe.wait_ge(h_ready, c + 1)
                        pe.wait_ge(txt_in[c], 16)
                        if c > 0:
                            pe.wait_ge(yt_ready, NL * c)
                        else:
                            pe.wait_ge(biasg_ready, 1)
                        src = h[:, c, :]
                    else:
                        pe.wait_ge(h2_ready, c + 1)
                        pe.wait_ge(pt0_copied, c + 1)
                        src = h2[:, c % 2, :]
                    pe.matmul(b5[:, 0:T], m("center"), src, start=True, stop=True).then_inc(xc_ready, 1)
                elif step == "ln_var":
                    pe.wait_ge(sq_ready, ln + 1)
                    if k == 0 and c > 0:
                        pe.wait_ge(hpre_ready, NL * c)
                    if k == 1:
                        pe.wait_ge(pt1_copied, c + 1)
                    pe.matmul(b6[:, 0:T], m("mean"), sq[:], start=True, stop=True).then_inc(var_ready, 1)
                elif step == "qkv":
                    pe.wait_ge(xn_ready, ln + 1)
                    if c > 0:
                        pe.wait_ge(out_ready, c)
                    pe.matmul(b6[:, 0:T], m("wqT"), xn[:], start=True, stop=True)
                    pe.matmul(b7[:, 0:T], m("wkT"), xn[:], start=True, stop=True).then_inc(qk_ready, 1)
                    for a in range(2):
                        mm = pe.matmul(b5[0:TT, P * a:P * (a + 1)], xn[:, TT * a:TT * (a + 1)], m("wvT"),
                                       start=True, stop=True)
                    mm.then_inc(v_ready, 1)
                elif step == "attn_scores":
                    pe.wait_ge(q_copied, c + 1)
                    pe.wait_ge(k_copied, c + 1)
                    for f in range(2):
                        for s in range(2):
                            mm = pe.matmul([b6, b7][f][0:TT, s * T:(s + 1) * T], QT[HALF[f], TT * s:TT * (s + 1)],
                                           KT[HALF[f], :], start=True, stop=True)
                        mm.then_inc(s_ready, 1)
                elif step == "attn_turn":
                    pe.wait_ge(v_copied, c + 1)
                    for f in range(2):
                        pe.wait_ge(p_ready, 4 * c + 2 * f + 2)
                        for s in range(2):
                            for t in range(2):
                                mm = pe.transpose([b5, b6][f][0:TT, T * t + TT * s:T * t + TT * (s + 1)],
                                                  Pr[:, f, s, TT * t:TT * (t + 1)], m("ident")[0:TT, 0:TT])
                        mm.then_inc(pt_ready, 1)
                elif step == "attn_apply":
                    pe.wait_ge(pt0_copied, c + 1)
                    pe.wait_ge(pt1_copied, c + 1)
                    for f in range(2):
                        for t in range(2):
                            mm = pe.matmul(b7[HALF[f], 0:T], V[:, t, D * f:D * (f + 1)], PT[:, f, t, :],
                                           start=(t == 0), stop=(t == 1))
                    mm.then_inc(pv_ready, 1)
                elif step == "expand":
                    pe.wait_ge(xn_ready, 2 * c + 2)
                    for f in range(2):
                        mm = pe.matmul(b7[:, T * f:T * (f + 1)], wiT[:, f, :], xn[:], start=True, stop=True)
                    mm.then_inc(expand_ready, 1)
                elif step == "experts":
                    pe.wait_ge(hid_relued, 3 * c + 1 + k)
                    if k == 0:
                        pe.wait_ge(group_selected, NL * GC * (c + 1))
                        pe.wait_ge(dve_zeroed, 3)
                    if k == 1:
                        pe.wait_ge(yt_ready, NL * c + 1)
                    for b in range(4):
                        for j in range(4):
                            g = 4 * b + j
                            mm = pe.matmul(b5[COLT * j:COLT * (j + 1), P * b:P * (b + 1)],
                                           hid[:, k, RG * g:RG * g + COLT], sel[:, c % 2, g, k, :],
                                           start=True, stop=True, tile_position=(0, COLT * j))
                    mm.then_inc(y_ready, 1)
                elif step == "experts_turn":
                    pe.wait_ge(yt_ready, NL * c + k + 1)
                    if k == 1:
                        pe.wait_ge(hpre_ready, NL * c + 1)
                    for b in range(4):
                        mm = pe.transpose(b6[:, P * b:P * (b + 1)], yt[:, b, :], m("ident"))
                    mm.then_inc(ytt_ready, 1)
                elif step == "project":
                    pe.wait_ge(hid_relued, 3 * c + 3)
                    for f in range(2):
                        mm = pe.matmul(b7[HALF[f], 0:T], m("woT"), hid[:, NL, T * f:T * (f + 1)], start=True, stop=True)
                    mm.then_inc(wo_ready, 1)


def kernel(**inputs):
    import numpy as np
    import concourse.bacc as bacc
    from concourse.bass_utils import run_bass_kernel_spmd

    a = {k: np.asarray(v) for k, v in inputs.items()}
    f32 = np.float32
    x = a["x"].reshape(C, 2, D, 8, 8, 8, 8)
    x = x.transpose(0, 1, 2, 3, 5, 4, 6).reshape(C, P, G, PIX)
    x_ch = np.ascontiguousarray(x.reshape(C, P, G * PIX))
    x_px = np.ascontiguousarray(
        x.reshape(C, P, G // 2, 2, PIX).transpose(0, 3, 4, 2, 1).reshape(C, P, G // 2, P))
    txt = np.ascontiguousarray(a["txt"].reshape(C, 2, TXT, D).transpose(0, 1, 3, 2).reshape(C, P, TXT))

    def twice(v):
        return np.concatenate([v, v], axis=0)

    def put(dst, at, v):
        dst[:v.shape[0], at[0]:at[0] + v.shape[1]] = v

    def diag2(v):
        out = np.zeros((P, P), f32)
        out[:D, :D] = v
        out[D:, D:] = v
        return out

    early = np.zeros((P, EARLY_N), f32)
    put(early, EARLY["wqT"], diag2(a["L0_tok_Wq"].T))
    put(early, EARLY["wk"], diag2(a["L0_tok_Wk"]))
    bk = np.zeros((2, NH, DH, NH, 2, NH), f32)
    for f in range(2):
        for hd in range(NH):
            bk[f, hd, :, :, f, hd] = a["L0_tok_bk"].reshape(NH, DH)[hd][:, None]
    put(early, EARLY["bk"], bk.reshape(P, P))
    put(early, EARLY["bq"], twice(a["L0_tok_bq"])[:, None])
    put(early, EARLY["bv"], twice(a["L0_tok_bv"])[:, None])
    put(early, EARLY["bo"], twice(a["L0_tok_bo"])[:, None])
    put(early, EARLY["head"], twice(np.repeat(np.eye(NH, dtype=f32), DH, axis=0)))
    put(early, EARLY["mask"], np.repeat(np.eye(NH, dtype=f32), SLOT, axis=0))

    mid = np.zeros((P, MID_N), f32)
    put(mid, MID["ident"], np.eye(P, dtype=f32))
    put(mid, MID["tvT"], diag2(a["L0_tok_Wv"].T))
    put(mid, MID["toT"], diag2(a["L0_tok_Wo"].T))
    put(mid, MID["center"], diag2(np.eye(D, dtype=f32) - f32(1.0 / D)))
    put(mid, MID["mean"], diag2(np.full((D, D), 1.0 / D, f32)))
    put(mid, MID["wqT"], diag2(a["L0_attn_Wq"].T))
    put(mid, MID["wkT"], diag2(a["L0_attn_Wk"].T))
    put(mid, MID["wvT"], diag2(a["L0_attn_Wv"].T))
    put(mid, MID["bq"], twice(a["L0_attn_bq"])[:, None])
    put(mid, MID["bk"], twice(a["L0_attn_bk"])[:, None])
    put(mid, MID["bv"], twice(a["L0_attn_bv"])[:, None])
    wi = np.zeros((P, 2, P), f32)
    wi[:D, 0] = a["L0_ffn_Wi"].T
    wi[D:, 1] = a["L0_ffn_Wi"].T
    put(mid, MID["wiT"], wi.reshape(P, 2 * P))
    put(mid, MID["bi"], a["L0_ffn_bi"][:, None])
    put(mid, MID["woT"], a["L0_ffn_Wo"].T)
    put(mid, MID["bo"], twice(a["L0_ffn_bo"])[:, None])
    br = np.zeros((P, NL, HID), f32)
    br[:NE] = a["L0_ffn_br"].transpose(1, 0, 2)
    br[NE] = a["L0_ffn_bs"][:, 0]
    put(mid, MID["brs"], br.reshape(P, NL * HID))
    rows = np.arange(P)
    put(mid, MID["expert"], np.where(rows < NE, rows, -1).astype(f32)[:, None])
    put(mid, MID["shared"], (rows == NE).astype(f32)[:, None])
    put(mid, MID["beta"], np.broadcast_to(a["L0_attn_beta"], (P, 2)))
    idx = np.arange(T, dtype=f32)
    dist = np.abs(idx[:, None] - idx[None, :])
    cosines = [np.cos(f32(2.0 * np.pi) * dist / f32(t)).astype(f32) for t in (24.0, 720.0)]
    cosines = np.stack(cosines).reshape(2, 2, TT, T).transpose(2, 0, 1, 3)
    put(mid, MID["cos"], cosines.reshape(TT, 2 * 2 * T))
    put(mid, MID["wsT"], a["L0_ffn_Ws"][:, 0].transpose(2, 0, 1).reshape(P, NL * HID))

    arrays = {
        "x_ch": x_ch, "x_px": x_px, "txt_ch": txt, "early_in_dram": early, "mid_in_dram": mid,
        "wrT_in": np.ascontiguousarray(a["L0_ffn_Wr"].transpose(3, 0, 1, 2)),
        "route_ids": np.ascontiguousarray(np.broadcast_to(a["L0_ffn_route_id"], (P, 64))),
    }
    nc = bacc.Bacc("TRN2", target_bir_lowering=False, num_devices=1)
    args = [nc.dram_tensor(n, v.shape, mybir.dt.from_np(v.dtype), kind="ExternalInput").ap() for n, v in arrays.items()]
    args.append(nc.dram_tensor("out_dram", (C, P, T), F32, kind="ExternalOutput").ap())
    early_fusion_kernel(nc, *args)
    r = run_bass_kernel_spmd(nc, [arrays], core_ids=[0])
    got = r.results[0]["out_dram"].reshape(C, 2, D, T).transpose(0, 1, 3, 2)
    return np.ascontiguousarray(got.reshape(B, T, D))
```

```python
from contextlib import ExitStack

import concourse.bass as bass
from concourse import mybir

F32 = mybir.dt.float32
I32 = mybir.dt.int32
ALU = mybir.AluOpType
ACT = mybir.ActivationFunctionType
AX = mybir.AxisListType.X

P = 128
D = 64
NH, DH = 8, 8
B = 8
C = B // 2
G = 64
PIX = 64
QUART = 16
GP = 32
SLOT = 2 * NH
COLT = 32
TXT = 128
T = G + TXT
TT = T // 2
QT_N = T // D
HID = 128
NE = 16
NL = 2
RG = B * T // 64
GC = 2 * T // RG
LN_EPS = 1e-5


def _columns(parts):
    at, out = 0, {}
    for name, n in parts:
        out[name] = (at, n)
        at += n
    return out, at


EARLY, EARLY_N = _columns([("wqT", P), ("wk", P), ("bk", P), ("bq", 1), ("bv", 1), ("bo", 1), ("head", NH), ("mask", NH)])
MID, MID_N = _columns([
    ("ident", P), ("wv_head", NH * COLT), ("toT", P), ("center", P), ("mean", P), ("wqT", P), ("wkT", P), ("wvT", P), ("bq", 1),
    ("bk", 1), ("bv", 1), ("wiT", P), ("bi", 1), ("woT", D), ("bo", 1), ("brs", NL * HID), ("expert", 1),
    ("shared", 1), ("beta", 2), ("wsT", NL * HID)])


def early_fusion_kernel(nc: bass.Bass, x_ch, x_px, txt, early_d, mid_d, cos_d, wrT_d, route_d, out):
    with ExitStack() as ctx:
        def sb(name, shape, dt=F32):
            return ctx.enter_context(nc.sbuf_tensor(name, shape, dt))

        def sem(name):
            return ctx.enter_context(nc.semaphore(name))

        xch = sb("xch", [P, 3, G * PIX])
        xpx = sb("xpx", [P, 2, G // 2, P])
        early = sb("early", [P, EARLY_N])
        mid = sb("mid", [P, MID_N])
        cos = sb("cos", [P, 2, QT_N, T])
        wrT = sb("wrT", [P, NE, NL, HID])
        sel = sb("sel", [P, 2, GC, NL, HID])
        wsI = sb("wsI", [P, NL, HID])
        route = sb("route", [P, 64], I32)
        onehot = sb("onehot", [P, 64])
        biasg = sb("biasg", [P, NL, 64])
        epsc = sb("epsc", [P, 1])
        cosb = sb("cosb", [P, QT_N, T])
        qsum = sb("qsum", [P, 2, G])
        qm = sb("qm", [P, 2, G])
        qp = sb("qp", [P, G])
        qph = sb("qph", [P, G, NH])
        R = sb("R", [P, 2, G, COLT])
        ck = sb("ck", [P, G])
        cc = sb("cc", [P, 2, 8])
        mx = sb("mx", [P, 8])
        sh = sb("sh", [P, 8])
        nsh = sb("nsh", [P, 8])
        bqs = sb("bqs", [P, 1])
        E = sb("E", [P, 8, PIX])
        den = sb("den", [P, 8])
        rden = sb("rden", [P, 8])
        AT = sb("AT", [P, G // 2, COLT])
        zc = sb("zc", [P, 8, P])
        Z = sb("Z", [P, G, NH])
        ctxv = sb("ctxv", [P, G])
        h = sb("h", [P, C, T])
        h2 = sb("h2", [P, 2, T])
        sq = sb("sq", [P, 2, T])
        lv = sb("lv", [P, 2, T])
        rstd = sb("rstd", [P, 2, T])
        xn = sb("xn", [P, 2, T])
        QT = sb("QT", [P, T])
        KT = sb("KT", [P, T])
        V = sb("V", [TT, 2, P])
        Pr = sb("Pr", [P, QT_N, T])
        nmx = sb("nmx", [P, QT_N])
        pden = sb("pden", [P, QT_N])
        prden = sb("prden", [P, QT_N])
        PT = sb("PT", [TT, QT_N, 2, P])
        hid = sb("hid", [P, NL + 1, 2, T + COLT - RG])
        yt = sb("yt", [P, 2, 2, HID])
        hpre = sb("hpre", [P, 2, GC // 2, RG])
        outT = sb("outT", [P, C, T])

        bank = [ctx.enter_context(nc.psum_tensor(f"bank{i}", [P, 512], F32)) for i in range(8)]
        bS, bR = bank[0], bank[1]
        bZ = [bank[2], bank[3]]
        bA, bB = bank[4], bank[5]
        bF, bG = bank[6], bank[7]

        x_ch_in = [[sem(f"x_ch_in{c}_{k}") for k in range(4)] for c in range(C)]
        x_px_in = [[sem(f"x_px_in{c}_{k}") for k in range(2)] for c in range(C)]
        txt_in = [sem(f"txt_in{c}") for c in range(C)]
        early_in, mid_in, cos_in, wr_in, route_in = (sem(n) for n in ("early_in", "mid_in", "cos_in", "wr_in", "route_in"))
        out_stored = [sem(f"out_stored{c}") for c in range(C)]
        dve_zeroed, pool_zeroed, onehot_ready, bias_part, cosb_ready, biasg_made, biasg_ready = (
            sem(n) for n in ("dve_zeroed", "pool_zeroed", "onehot_ready", "bias_part", "cosb_ready", "biasg_made", "biasg_ready"))
        wsi_ready, group_selected = (sem(n) for n in ("wsi_ready", "group_selected"))
        qsum_ready, q_ready, qp_made, qp_ready, qph_ready, c_made, r_ready, r_lo_copied, r_hi_copied, ck_masked, cc_ready = (
            sem(n) for n in ("qsum_ready", "q_ready", "qp_made", "qp_ready", "qph_ready", "c_made", "r_ready",
                             "r_lo_copied", "r_hi_copied", "ck_masked", "cc_ready"))
        scores_ready, mx_ready, sh_ready, nsh_ready, exp_ready, bqs_ready = (
            sem(n) for n in ("scores_ready", "mx_ready", "sh_ready", "nsh_ready", "exp_ready", "bqs_ready"))
        rden_ready, attn_ready, attnT_ready, at_lo_copied, at_hi_copied = (
            sem(n) for n in ("rden_ready", "attn_ready", "attnT_ready", "at_lo_copied", "at_hi_copied"))
        z_ready, zc_ready, zt_ready, z_lo_copied, z_hi_copied, ctx_ready, ctxv_ready, tok_ready, h_ready = (
            sem(n) for n in ("z_ready", "zc_ready", "zt_ready", "z_lo_copied", "z_hi_copied", "ctx_ready",
                             "ctxv_ready", "tok_ready", "h_ready"))
        xc_ready, sq_ready, var_ready, lv_ready, rstd_ready, xn_ready = (
            [sem(f"{n}{stage}") for stage in range(2)]
            for n in ("xc_ready", "sq_ready", "var_ready", "lv_ready", "rstd_ready", "xn_ready"))
        qk_ready, v_ready, qk_copied, v_copied, s_ready, biased, pexp_ready = (
            sem(n) for n in ("qk_ready", "v_ready", "qk_copied", "v_copied", "s_ready", "biased", "pexp_ready"))
        prden_ready, p_ready, pt_ready, pt0_copied, pt1_copied, pv_ready, h2_ready = (
            sem(n) for n in ("prden_ready", "p_ready", "pt_ready", "pt0_copied", "pt1_copied", "pv_ready", "h2_ready"))
        expand_ready, y_ready, yt_ready, ytt_ready, hpre_ready, hid_relued, wo_ready, out_ready = (
            sem(n) for n in ("expand_ready", "y_ready", "yt_ready", "ytt_ready", "hpre_ready", "hid_relued", "wo_ready", "out_ready"))

        def e(name, rows=slice(0, P)):
            at, n = EARLY[name]
            return early[rows, at:at + n]

        def m(name, rows=slice(0, P)):
            at, n = MID[name]
            return mid[rows, at:at + n]

        HALF = [slice(0, D), slice(D, P)]
        RELUS = 2 + 2 * NL
        INV = float(DH) ** -0.5
        brs = m("brs").rearrange("p (l n) -> p l n", l=NL)
        wsT = m("wsT").rearrange("p (l n) -> p l n", l=NL)
        wv_head = m("wv_head").rearrange("p (h n) -> p h n", h=NH)

        def att_scores(t):
            return [bB[:, 0:T], bB[:, T:2 * T], bA[:, 0:T]][t]

        def att_turned(t):
            return [bB[0:TT, 0:2 * P], bB[0:TT, 2 * P:], bA[0:TT, 0:2 * P]][t]

        def r_src(f, slot):
            return bR[:, 0:GP * NH].rearrange("p (m k s h) -> p m k s h", k=2, s=2, h=NH)[HALF[f], :, slot]

        def r_dst(c, k, f, slot):
            at = SLOT * slot + NH * f
            return R[:, c % 2, GP * k:GP * (k + 1)].rearrange("p (m k s) n -> p m k s n", k=2, s=2)[HALF[f], :, slot, :, at:at + NH]

        def at_src(sp):
            return bS[:].rearrange("p (g f h) -> p g f h", f=2, h=NH)[HALF[sp]]

        def at_dst(sp):
            return AT[:].rearrange("p g (f s h) -> p g f s h", f=2, s=2)[HALF[sp], :, :, sp]

        def zt_src(n, f):
            return bZ[n][:].rearrange("p (q k j f e) -> p q k j f e", q=2, k=2, j=4, f=2)[HALF[f], :, :, :, f]

        def zt_dst(n, f):
            return Z[:].rearrange("p (n q j k s) h -> p n q k j (s h)", n=2, q=2, j=4, k=2)[HALF[f], n]

        START = {
            "queries": (0, 2288, 4553, 7252),
            "patches": (235, 2301, 4485, 7291),
            "attention": (245, 2381, 4556, 7285),
            "ffn": (231, 2346, 4494, 7131),
        }
        PHASE = {
            "queries": (
                "qp", "r", "c", "r_copy", "pool", "mean", "qp_copy", "qp_spread", "c_mask", "c_pick"),
            "patches": (
                "scores", "turn", "z", "zturn", "context", "tokens", "exp", "turn_copy", "z_copy", "zturn_copy",
                "shift", "normalise", "context_add", "tokens_add"),
            "attention": (
                "qk", "v", "attn_scores", "attn_turn", "attn_apply", "qk_copy", "v_copy", "attn_exp",
                "attn_turn_copy", "attn_bias", "attn_norm", "attn_add"),
            "ffn": (
                "setup", "expand", "experts", "yturn", "project", "expand_relu", "y_copy", "y_relu", "y_bias",
                "output"),
        }
        PHASE_OF = {step: phase for phase, steps in PHASE.items() for step in steps}
        PLACE = {
            "PE": [
                ("qp", 0, -1027), ("r", 0, -736), ("qp", 1, -466), ("scores", 0, -202), ("r", 1, -206),
                ("scores", 1, -187), ("scores", 2, -37), ("scores", 3, -37), ("c", 0, 158), ("scores", 4, 329),
                ("scores", 5, 444), ("scores", 6, 458), ("scores", 7, 474), ("turn", 0, 1173), ("turn", 1, 1209),
                ("z", 0, 1572), ("z", 1, 1659), ("z", 2, 1926), ("z", 3, 1952), ("setup", 0, 1912),
                ("zturn", 0, 2281), ("zturn", 1, 2413), ("context", 0, 2538), ("tokens", 0, 2670),
                ("ln_center", 0, 2923), ("ln_var", 0, 3076), ("qk", 0, 3188), ("v", 0, 3346),
                ("attn_scores", 0, 3397), ("attn_scores", 1, 3698), ("attn_turn", 0, 4283), ("attn_turn", 1, 4284),
                ("attn_turn", 2, 4433), ("attn_apply", 0, 4857), ("ln_center", 1, 5471), ("ln_var", 1, 5763),
                ("expand", 0, 6012), ("expand", 1, 6025), ("experts", 0, 6276), ("experts", 1, 6280),
                ("yturn", 0, 6318), ("yturn", 1, 6641), ("experts", 2, 6784), ("experts", 3, 6963),
                ("yturn", 2, 6994), ("yturn", 3, 7166), ("project", 0, 7436), ("project", 1, 7515)],
            "ACT": [
                ("r_copy", 0, -643), ("r_copy", 1, 44), ("exp", 0, 839), ("exp", 1, 955), ("turn_copy", 0, 1355),
                ("z_copy", 0, 1921), ("z_copy", 1, 1971), ("zturn_copy", 0, 2347), ("zturn_copy", 1, 2378),
                ("ln_square", 0, 2872), ("ln_log", 0, 2994), ("ln_rstd", 0, 2997), ("qk_copy", 0, 3229),
                ("v_copy", 0, 3302), ("attn_exp", 0, 3834), ("attn_exp", 1, 4053), ("attn_exp", 2, 4195),
                ("attn_turn_copy", 0, 4643), ("ln_square", 1, 5458), ("ln_log", 1, 5803), ("ln_rstd", 1, 5859),
                ("expand_relu", 0, 6088), ("y_copy", 0, 6238), ("expand_relu", 1, 6219), ("y_copy", 1, 6423),
                ("y_relu", 0, 6690), ("y_relu", 1, 6696), ("y_copy", 2, 6851), ("y_copy", 3, 6991),
                ("y_relu", 2, 7240), ("y_relu", 3, 7456)],
            "DVE": [
                ("pool", 0, -2250), ("pool", 1, -1382), ("pool", 2, -1181), ("mean", 0, -1314), ("pool", 3, -1096),
                ("qp_copy", 0, -1002), ("qp_spread", 0, -947), ("r_copy", 0, -726), ("mean", 1, -697),
                ("qp_copy", 1, -493), ("qp_spread", 1, -474), ("r_copy", 1, -4), ("c_mask", 0, 194),
                ("c_pick", 0, 272), ("shift", 0, 652), ("normalise", 0, 1035), ("normalise", 1, 1042),
                ("turn_copy", 0, 1291), ("setup", 0, 1978), ("zturn_copy", 0, 2265), ("zturn_copy", 1, 2467),
                ("context_add", 0, 2655), ("tokens_add", 0, 2709), ("ln_scale", 0, 2960), ("attn_bias", 0, 3621),
                ("attn_bias", 1, 3728), ("attn_bias", 2, 3964), ("attn_norm", 0, 4010), ("attn_norm", 1, 4029),
                ("attn_norm", 2, 4184), ("attn_turn_copy", 1, 4606), ("attn_add", 0, 4902), ("ln_scale", 1, 5834),
                ("y_bias", 0, 6600), ("y_bias", 1, 6755), ("y_bias", 2, 6946), ("y_bias", 3, 7159),
                ("output", 0, 7527), ("output", 1, 7642)],
        }

        def start(step, part, c):
            return START[PHASE_OF.get(step) or ("attention", "ffn")[part]][c]

        SCHEDULE = {
            engine: sorted(((step, c, part) for c in range(C) for step, part, _ in steps if step != "setup" or c == 0),
                           key=lambda s: start(s[0], s[2], s[1]) + {(n, p): at for n, p, at in steps}[s[0], s[2]])
            for engine, steps in PLACE.items()}

        block = ctx.enter_context(nc.Block())

        @block.sync
        def _(sp):
            def load_ch(c):
                if c >= 3:
                    sp.wait_ge(scores_ready, c - 2)
                for k in range(4):
                    cols = slice(k * QUART * PIX, (k + 1) * QUART * PIX)
                    sp.dma_start(xch[:, c % 3, cols], x_ch[c, :, cols]).then_inc(x_ch_in[c][k], 16)

            def load_px(c):
                if c >= 2:
                    sp.wait_ge(z_ready, 2 * (c - 1))
                for k in range(2):
                    gp = slice(k * G // 4, (k + 1) * G // 4)
                    sp.dma_start(xpx[:, c % 2, gp, :], x_px[c, :, gp, :]).then_inc(x_px_in[c][k], 16)

            load_ch(0)
            sp.dma_start(route[:], route_d).then_inc(route_in, 16)
            sp.dma_start(mid[:], mid_d).then_inc(mid_in, 16)
            load_ch(1)
            load_px(0)
            sp.dma_start(cos[:], cos_d).then_inc(cos_in, 16)
            load_ch(2)
            load_px(1)
            for c in range(C):
                sp.dma_start(h[:, c, G:T], txt[c]).then_inc(txt_in[c], 16)
            sp.dma_start(wrT[:], wrT_d).then_inc(wr_in, 16)
            load_ch(3)
            load_px(2)
            load_px(3)
            for c in range(C):
                sp.wait_ge(out_ready, 2 * (c + 1))
                sp.dma_start(out[c], outT[:, c, :]).then_inc(out_stored[c], 16)
            for c in range(C):
                sp.wait_ge(out_stored[c], 16)

        @block.gpsimd
        def _(pool):
            pool.memset(R[:, 1], 0.0).then_inc(pool_zeroed, 1)
            pool.memset(AT[:], 0.0).then_inc(pool_zeroed, 1)
            pool.wait_ge(mid_in, 16)
            for l in range(NL):
                pool.tensor_tensor(wsI[:, l, :], wsT[:, l, :], m("ident"), ALU.add).then_inc(wsi_ready, 1)
            pool.wait_ge(wsi_ready, NL)
            pool.wait_ge(wr_in, 16)
            pool.wait_ge(route_in, 16)
            for c in range(C):
                if c >= 2:
                    pool.wait_ge(y_ready, 2 * NL * (c - 1))
                with pool.Fori(0, GC // 4) as b:
                    experts = [pool.value_load(route[0:1].rearrange("p (b i) -> p b i", i=4)[:, bass.ds(b + GC // 4 * c, 1), i],
                                               min_val=0, max_val=NE - 1) for i in range(4)]
                    for i, ex in enumerate(experts):
                        pool.tensor_tensor(sel[:, c % 2].rearrange("p (b i) l n -> p b i l n", i=4)[:, bass.ds(b, 1), i],
                                           wrT[:, bass.ds(ex, 1)], wsI[:].rearrange("p (o l) n -> p o l n", o=1),
                                           ALU.add).then_inc(group_selected, 1)

        @block.scalar
        def _(act):
            act.dma_start(early[:], early_d).then_inc(early_in, 16)
            act.preload_act_table_set("natural_log_exp_and_others")

            for step, c, k in SCHEDULE["ACT"]:
                if step == "r_copy":
                    act.wait_ge(r_ready, 2 * c + k + 1)
                    if c == 0:
                        act.wait_ge(dve_zeroed, 2)
                    if c == 1:
                        act.wait_ge(pool_zeroed, 1)
                    for slot in range(2):
                        act.activation(r_dst(c, k, 0, slot), r_src(0, slot), ACT.Copy).then_inc(r_lo_copied, 1)
                elif step == "exp":
                    act.wait_ge(nsh_ready, c + 1)
                    if c > 0:
                        act.wait_ge(attnT_ready, 2 * c)
                    for s in range(4 * k, 4 * k + 4):
                        act.activation(E[:, s, :], bS[:, PIX * s:PIX * (s + 1)], ACT.Exp, bias=nsh[:, s:s + 1],
                                       accum_out=den[:, s:s + 1]).then_inc(exp_ready, 1)
                elif step == "turn_copy":
                    act.wait_ge(attnT_ready, 2 * (c + 1))
                    if c == 0:
                        act.wait_ge(pool_zeroed, 2)
                    if c > 0:
                        act.wait_ge(z_ready, 2 * c)
                    act.activation(at_dst(0), at_src(0), ACT.Copy).then_inc(at_lo_copied, 1)
                elif step == "z_copy":
                    act.wait_ge(z_ready, 2 * c + k + 1)
                    if c > 0:
                        act.wait_ge(zt_ready, 2 * c)
                    act.activation(zc[:, 4 * k:4 * k + 4, :], bZ[k][:].rearrange("p (q n) -> p q n", q=4),
                                   ACT.Copy).then_inc(zc_ready, 1)
                elif step == "zturn_copy":
                    act.wait_ge(zt_ready, 2 * c + k + 1)
                    if c > 0:
                        act.wait_ge(ctx_ready, c)
                    for q in range(2):
                        act.activation(zt_dst(k, 0)[:, q], zt_src(k, 0)[:, q], ACT.Copy).then_inc(z_lo_copied, 1)
                elif step == "ln_square":
                    act.wait_ge(xc_ready[k], c + 1)
                    act.activation(sq[:, k], [bA, bF][k][:, 0:T], ACT.Square).then_inc(sq_ready[k], 1)
                elif step == "ln_log":
                    act.wait_ge(var_ready[k], c + 1)
                    if c == 0:
                        act.wait_ge(dve_zeroed, 1)
                    act.activation(lv[:, k], [bB, bG][k][:, 0:T], ACT.Ln, bias=epsc[:, 0:1]).then_inc(lv_ready[k], 1)
                elif step == "ln_rstd":
                    act.wait_ge(lv_ready[k], c + 1)
                    if c > 0:
                        act.wait_ge(xn_ready[k], c)
                    act.activation(rstd[:, k], lv[:, k], ACT.Exp, scale=-0.5).then_inc(rstd_ready[k], 1)
                elif step == "qk_copy":
                    act.wait_ge(qk_ready, c + 1)
                    if c == 0:
                        act.wait_ge(bqs_ready, 1)
                    act.activation(QT[:], bB[:, 0:T], ACT.Identity, bias=bqs[:, 0:1], scale=float(D) ** -0.5).then_inc(qk_copied, 1)
                    act.activation(KT[:], bB[:, T:2 * T], ACT.Identity, bias=m("bk")).then_inc(qk_copied, 1)
                elif step == "v_copy":
                    act.wait_ge(v_ready, c + 1)
                    act.activation(V[:], bA[0:TT, 0:2 * P].rearrange("p (a n) -> p a n", a=2),
                                   ACT.Copy).then_inc(v_copied, 1)
                elif step == "attn_exp":
                    act.wait_ge(biased, QT_N * c + k + 1)
                    act.activation(Pr[:, k, :], Pr[:, k, :], ACT.Exp, bias=nmx[:, k:k + 1], scale=-1.0,
                                   accum_out=pden[:, k:k + 1]).then_inc(pexp_ready, 1)
                elif step == "attn_turn_copy" and k == 0:
                    act.wait_ge(pt_ready, QT_N * c + 2)
                    act.activation(PT[:, 0:2], bB[0:TT].rearrange("p (a t q) -> p a t q", a=2, t=2),
                                   ACT.Copy).then_inc(pt0_copied, 1)
                elif step == "expand_relu":
                    act.wait_ge(expand_ready, 2 * c + k + 1)
                    act.activation(hid[:, 0, k, 0:T], [bF, bG][k][:, 0:T], ACT.Relu, bias=m("bi")).then_inc(hid_relued, 1)
                elif step == "y_copy":
                    l, f = k // 2, k % 2
                    act.wait_ge(y_ready, 2 * NL * c + k + 1)
                    if c + l > 0:
                        act.wait_ge(ytt_ready, 2 * NL * c + k - 1)
                    act.activation(yt[:, f], [bF, bG][f][:, 0:2 * P].rearrange("p (b n) -> p b n", b=2),
                                   ACT.Copy).then_inc(yt_ready, 1)
                elif step == "y_relu":
                    act.wait_ge(hpre_ready, 2 * NL * c + k + 1)
                    act.activation(hid[:, k // 2 + 1, k % 2, 0:T], hpre[:, k % 2].rearrange("p g n -> p (g n)"),
                                   ACT.Relu).then_inc(hid_relued, 1)

        @block.vector
        def _(dve):
            dve.memset(epsc[:], LN_EPS).then_inc(dve_zeroed, 1)
            dve.memset(R[:, 0], 0.0).then_inc(dve_zeroed, 1)
            dve.memset(hid[:, :, :, T:], 0.0).then_inc(dve_zeroed, 1)
            dve.wait_ge(early_in, 16)

            for step, c, k in SCHEDULE["DVE"]:
                if step == "pool":
                    dve.wait_ge(x_ch_in[c][k], 16)
                    dve.tensor_reduce(qsum[:, c % 2, QUART * k:QUART * (k + 1)],
                                      xch[:, c % 3, QUART * PIX * k:QUART * PIX * (k + 1)]
                                      .rearrange("p (g n) -> p g n", n=PIX), AX, ALU.add).then_inc(qsum_ready, 1)
                elif step == "mean":
                    dve.wait_ge(qsum_ready, 4 * c + 2 * (k + 1))
                    GS = slice(GP * k, GP * (k + 1))
                    dve.tensor_scalar(qm[:, c % 2, GS], qsum[:, c % 2, GS], 1.0 / PIX, None, ALU.mult).then_inc(q_ready, 1)
                elif step == "qp_copy":
                    dve.wait_ge(qp_made, 2 * c + k + 1)
                    if c > 0:
                        dve.wait_ge(c_made, c)
                    dve.tensor_scalar(qp[:, GP * k:GP * (k + 1)], bR[:, 0:GP], e("bq"), INV, ALU.add, ALU.mult).then_inc(qp_ready, 1)
                elif step == "qp_spread":
                    dve.wait_ge(qp_ready, 2 * c + k + 1)
                    if c > 0:
                        dve.wait_ge(r_ready, 2 * c)
                    dve.tensor_tensor(qph[:, GP * k:GP * (k + 1)],
                                      qp[:, GP * k:GP * (k + 1)].rearrange("p (g o) -> p g o", o=1).to_broadcast([P, GP, NH]),
                                      e("head").rearrange("p (o h) -> p o h", o=1).to_broadcast([P, GP, NH]),
                                      ALU.mult).then_inc(qph_ready, 1)
                elif step == "r_copy":
                    dve.wait_ge(r_ready, 2 * c + k + 1)
                    if c == 1:
                        dve.wait_ge(pool_zeroed, 1)
                    for slot in range(2):
                        dve.tensor_copy(r_dst(c, k, 1, slot), r_src(1, slot)).then_inc(r_hi_copied, 1)
                elif step == "c_mask":
                    dve.wait_ge(c_made, c + 1)
                    dve.tensor_tensor(ck[:].rearrange("p (q n s) -> p q n s", q=4, s=2),
                                      bR[:, 0:G].rearrange("p (q n s) -> p q n s", q=4, s=2),
                                      e("mask").rearrange("p (o n q) -> p o n q", o=1, q=1).to_broadcast([P, 4, NH, 2]),
                                      ALU.mult).then_inc(ck_masked, 1)
                elif step == "c_pick":
                    dve.wait_ge(ck_masked, c + 1)
                    dve.tensor_reduce(cc[:, c % 2].rearrange("p (q s) -> p q s", s=2),
                                      ck[:].rearrange("p (q n s) -> p q s n", q=4, s=2), AX, ALU.add).then_inc(cc_ready, 1)
                elif step == "setup":
                    dve.wait_ge(mid_in, 16)
                    dve.wait_ge(route_in, 16)
                    dve.tensor_scalar(onehot[:], route[:], m("expert"), m("shared"), ALU.is_equal,
                                      ALU.add).then_inc(onehot_ready, 1)
                    dve.wait_ge(cos_in, 16)
                    dve.tensor_scalar(cosb[:], cos[:, 0], m("beta")[:, 0:1], None, ALU.mult).then_inc(bias_part, 1)
                    dve.wait_ge(bias_part, 1)
                    dve.scalar_tensor_tensor(out=cosb[:], in0=cos[:, 1], scalar=m("beta")[:, 1:2], in1=cosb[:],
                                             op0=ALU.mult, op1=ALU.add).then_inc(cosb_ready, 1)
                    dve.tensor_scalar(bqs[:], m("bq"), float(D) ** -0.5, None, ALU.mult).then_inc(bqs_ready, 1)
                    dve.wait_ge(biasg_made, 1)
                    dve.tensor_copy(biasg[:], bF[:, 0:NL * 64].rearrange("p (l g) -> p l g", l=NL)).then_inc(biasg_ready, 1)
                elif step == "shift":
                    S = bS[:].rearrange("p (s n) -> p s n", n=PIX)
                    dve.wait_ge(scores_ready, c + 1)
                    dve.tensor_reduce(mx[:], S, AX, ALU.max).then_inc(mx_ready, 1)
                    dve.wait_ge(mx_ready, c + 1)
                    dve.wait_ge(cc_ready, c + 1)
                    dve.tensor_tensor(sh[:], mx[:], cc[:, c % 2], ALU.add).then_inc(sh_ready, 1)
                    dve.wait_ge(sh_ready, c + 1)
                    if c > 0:
                        dve.wait_ge(exp_ready, 8 * c)
                    dve.tensor_tensor(nsh[:], cc[:, c % 2], sh[:], ALU.subtract).then_inc(nsh_ready, 1)
                elif step == "normalise":
                    SS = slice(4 * k, 4 * k + 4)
                    dve.wait_ge(exp_ready, 8 * c + 4 * (k + 1))
                    dve.reciprocal(rden[:, SS], den[:, SS]).then_inc(rden_ready, 1)
                    dve.wait_ge(rden_ready, 2 * c + k + 1)
                    dve.tensor_tensor(E[:, SS], E[:, SS], rden[:, SS].rearrange("p (s o) -> p s o", o=1)
                                      .to_broadcast([P, 4, PIX]), ALU.mult).then_inc(attn_ready, 1)
                elif step == "turn_copy":
                    dve.wait_ge(attnT_ready, 2 * (c + 1))
                    if c == 0:
                        dve.wait_ge(pool_zeroed, 2)
                    if c > 0:
                        dve.wait_ge(z_ready, 2 * c)
                    dve.tensor_copy(at_dst(1), at_src(1)).then_inc(at_hi_copied, 1)
                elif step == "zturn_copy":
                    dve.wait_ge(zt_ready, 2 * c + k + 1)
                    if c > 0:
                        dve.wait_ge(ctx_ready, c)
                    for q in range(2):
                        dve.tensor_copy(zt_dst(k, 1)[:, q], zt_src(k, 1)[:, q]).then_inc(z_hi_copied, 1)
                elif step == "context_add":
                    dve.wait_ge(ctx_ready, c + 1)
                    dve.tensor_scalar(ctxv[:], bZ[0][:, 0:G], e("bv"), None, ALU.add).then_inc(ctxv_ready, 1)
                elif step == "tokens_add":
                    dve.wait_ge(tok_ready, c + 1)
                    dve.scalar_tensor_tensor(out=h[:, c, 0:G], in0=bZ[1][:, 0:G], scalar=e("bo"), in1=qm[:, c % 2, :],
                                             op0=ALU.add, op1=ALU.add).then_inc(h_ready, 1)
                elif step == "ln_scale":
                    dve.wait_ge(rstd_ready[k], c + 1)
                    dve.tensor_tensor(xn[:, k], [bA, bF][k][:, 0:T], rstd[:, k], ALU.mult).then_inc(xn_ready[k], 1)
                elif step == "attn_bias":
                    dve.wait_ge(s_ready, 2 * c + k // 2 + 1)
                    if k == 0 and c == 0:
                        dve.wait_ge(cosb_ready, 1)
                    dve.tensor_tensor_reduce(Pr[:, k, :], att_scores(k), cosb[:, k, :],
                                             -1.0, 3.0e38, ALU.add, ALU.min, nmx[:, k:k + 1]).then_inc(biased, 1)
                elif step == "attn_norm":
                    dve.wait_ge(pexp_ready, QT_N * c + k + 1)
                    dve.reciprocal(prden[:, k:k + 1], pden[:, k:k + 1]).then_inc(prden_ready, 1)
                    dve.wait_ge(prden_ready, QT_N * c + k + 1)
                    dve.tensor_scalar(Pr[:, k, :], Pr[:, k, :], prden[:, k:k + 1], None, ALU.mult).then_inc(p_ready, 1)
                elif step == "attn_turn_copy" and k == 1:
                    dve.wait_ge(pt_ready, QT_N * (c + 1))
                    dve.tensor_copy(PT[:, 2], att_turned(2).rearrange("p (t q) -> p t q", t=2)).then_inc(pt1_copied, 1)
                elif step == "attn_add":
                    dve.wait_ge(pv_ready, c + 1)
                    dve.scalar_tensor_tensor(out=h2[:, c % 2, :], in0=bB[:, 0:T], scalar=m("bv"), in1=h[:, c, :],
                                             op0=ALU.add, op1=ALU.add).then_inc(h2_ready, 1)
                elif step == "y_bias":
                    l, f = k // 2, k % 2
                    dve.wait_ge(ytt_ready, 2 * NL * c + k + 1)
                    if c + l > 0:
                        dve.wait_ge(hid_relued, RELUS * c + k + 1 if l else RELUS * c - 1 + f)
                    if c + k == 0:
                        dve.wait_ge(biasg_ready, 1)
                    at = GC * c + GC // 2 * f
                    dve.tensor_tensor(hpre[:, f], [bF, bG][f][:, 2 * P:].rearrange("p (g n) -> p g n", n=COLT)[:, :, 0:RG],
                                      biasg[:, l, at:at + GC // 2].rearrange("p (g o) -> p g o", o=1)
                                      .to_broadcast([P, GC // 2, RG]), ALU.add).then_inc(hpre_ready, 1)
                elif step == "output":
                    dve.wait_ge(wo_ready, 2 * c + k + 1)
                    dve.scalar_tensor_tensor(out=outT[HALF[k], c, :], in0=[bF, bG][k][HALF[k], 0:T], scalar=m("bo", HALF[k]),
                                             in1=h2[HALF[k], c % 2, :], op0=ALU.add, op1=ALU.add).then_inc(out_ready, 1)

        @block.tensor
        def _(pe):
            for step, c, k in SCHEDULE["PE"]:
                if step == "qp":
                    pe.wait_ge(q_ready, 2 * c + k + 1)
                    if c + k == 0:
                        pe.wait_ge(early_in, 16)
                    if k == 0 and c > 0:
                        pe.wait_ge(ck_masked, c)
                    if k == 1:
                        pe.wait_ge(r_lo_copied, 4 * c + 2)
                        pe.wait_ge(r_hi_copied, 4 * c + 2)
                    pe.matmul(bR[:, 0:GP], e("wqT"), qm[:, c % 2, GP * k:GP * (k + 1)], start=True, stop=True).then_inc(qp_made, 1)
                elif step == "r":
                    pe.wait_ge(qph_ready, 2 * c + k + 1)
                    pe.matmul(bR[:, 0:GP * NH], e("wk"), qph[:, GP * k:GP * (k + 1)].rearrange("p g h -> p (g h)"),
                              start=True, stop=True).then_inc(r_ready, 1)
                elif step == "c":
                    pe.wait_ge(r_lo_copied, 4 * (c + 1))
                    pe.wait_ge(r_hi_copied, 4 * (c + 1))
                    pe.matmul(bR[:, 0:G], e("bk"), qp[:], start=True, stop=True).then_inc(c_made, 1)
                elif step == "scores":
                    if k % 4 == 0:
                        pe.wait_ge(r_lo_copied, 4 * c + 2 * (k // 4 + 1))
                        pe.wait_ge(r_hi_copied, 4 * c + 2 * (k // 4 + 1))
                    if k == 0:
                        if c > 0:
                            pe.wait_ge(at_lo_copied, c)
                            pe.wait_ge(at_hi_copied, c)
                    q, s = k // 2, k % 2
                    if s == 0:
                        pe.wait_ge(x_ch_in[c][q], 16)
                    for slot in range(2):
                        for j in range(4):
                            g = 16 * q + 4 * j + 2 * slot + s
                            mm = pe.matmul(bS[COLT * j:COLT * (j + 1), PIX * k:PIX * (k + 1)],
                                           R[:, c % 2, g, :], xch[:, c % 3, PIX * g:PIX * (g + 1)],
                                           start=(k == 0 and slot == 0), stop=(slot == 1),
                                           skip_group_check=True, tile_position=(0, COLT * j))
                    if k == 7:
                        mm.then_inc(scores_ready, 1)
                elif step == "turn":
                    pe.wait_ge(attn_ready, 2 * c + k + 1)
                    if k == 0:
                        pe.wait_ge(exp_ready, 8 * (c + 1))
                        if c == 0:
                            pe.wait_ge(mid_in, 16)
                    for q in (2 * k, 2 * k + 1):
                        mm = pe.transpose(bS[:, P * q:P * (q + 1)],
                                          E[:, 2 * q:2 * q + 2, :].rearrange("p s n -> p (s n)"), m("ident"))
                    mm.then_inc(attnT_ready, 1)
                elif step == "z":
                    if k == 0:
                        pe.wait_ge(at_lo_copied, c + 1)
                        pe.wait_ge(at_hi_copied, c + 1)
                        if c > 0:
                            pe.wait_ge(ctxv_ready, c)
                    if k == 2 and c > 0:
                        pe.wait_ge(h_ready, c)
                    if k % 2 == 0:
                        pe.wait_ge(x_px_in[c][k // 2], 16)
                    for slot in range(2):
                        for j in range(4):
                            gp = 8 * k + 2 * j + slot
                            at = P * (2 * (k % 2) + slot)
                            mm = pe.matmul(bZ[k // 2][COLT * j:COLT * (j + 1), at:at + P], AT[:, gp, :],
                                           xpx[:, c % 2, gp, :], start=True, stop=True, tile_position=(0, COLT * j))
                    if k % 2:
                        mm.then_inc(z_ready, 1)
                elif step == "zturn":
                    pe.wait_ge(zc_ready, 2 * c + k + 1)
                    for q in range(4):
                        mm = pe.transpose(bZ[k][:, P * q:P * (q + 1)], zc[:, 4 * k + q, :], m("ident"))
                    mm.then_inc(zt_ready, 1)
                elif step == "context":
                    pe.wait_ge(z_lo_copied, 4 * (c + 1))
                    pe.wait_ge(z_hi_copied, 4 * (c + 1))
                    for i in range(4):
                        for f in range(2):
                            for t in range(2):
                                hd = 4 * t + i
                                mm = pe.matmul(bZ[0][D * f + COLT * t:D * f + COLT * (t + 1), 0:G],
                                               wv_head[HALF[f], hd, :], Z[HALF[f], :, hd], start=(i == 0), stop=(i == 3),
                                               skip_group_check=True, tile_position=(D * f, D * f + COLT * t))
                    mm.then_inc(ctx_ready, 1)
                elif step == "tokens":
                    pe.wait_ge(ctxv_ready, c + 1)
                    pe.matmul(bZ[1][:, 0:G], m("toT"), ctxv[:], start=True, stop=True).then_inc(tok_ready, 1)
                elif step == "setup":
                    pe.wait_ge(onehot_ready, 1)
                    for l in range(NL):
                        mm = pe.matmul(bF[:, 64 * l:64 * (l + 1)], brs[:, l, :], onehot[:], start=True, stop=True)
                    mm.then_inc(biasg_made, 1)
                elif step == "ln_center":
                    if k == 0:
                        pe.wait_ge(h_ready, c + 1)
                        pe.wait_ge(txt_in[c], 16)
                        if c > 0:
                            pe.wait_ge(pt1_copied, c)
                        pe.matmul(bA[:, 0:T], m("center"), h[:, c, :], start=True, stop=True).then_inc(xc_ready[0], 1)
                    else:
                        pe.wait_ge(h2_ready, c + 1)
                        if c > 0:
                            pe.wait_ge(out_ready, 2 * c)
                        else:
                            pe.wait_ge(biasg_ready, 1)
                        pe.matmul(bF[:, 0:T], m("center"), h2[:, c % 2, :], start=True, stop=True).then_inc(xc_ready[1], 1)
                elif step == "ln_var":
                    pe.wait_ge(sq_ready[k], c + 1)
                    if k == 0 and c > 0:
                        pe.wait_ge(h2_ready, c)
                    pe.matmul([bB, bG][k][:, 0:T], m("mean"), sq[:, k], start=True, stop=True).then_inc(var_ready[k], 1)
                elif step == "qk":
                    pe.wait_ge(xn_ready[0], c + 1)
                    pe.matmul(bB[:, 0:T], m("wqT"), xn[:, 0], start=True, stop=True)
                    pe.matmul(bB[:, T:2 * T], m("wkT"), xn[:, 0], start=True, stop=True).then_inc(qk_ready, 1)
                elif step == "v":
                    pe.wait_ge(xn_ready[0], c + 1)
                    for a in range(2):
                        mm = pe.matmul(bA[0:TT, P * a:P * (a + 1)], xn[:, 0, TT * a:TT * (a + 1)], m("wvT"),
                                       start=True, stop=True)
                    mm.then_inc(v_ready, 1)
                elif step == "attn_scores":
                    pe.wait_ge(qk_copied, 2 * (c + 1))
                    if k == 1:
                        pe.wait_ge(v_copied, c + 1)
                    for t in ([0, 1], [2])[k]:
                        for f in range(2):
                            mm = pe.matmul(att_scores(t)[HALF[f]], QT[HALF[f], D * t:D * (t + 1)], KT[HALF[f], :],
                                           start=True, stop=True, tile_position=(D * f, D * f))
                    mm.then_inc(s_ready, 1)
                elif step == "attn_turn":
                    pe.wait_ge(p_ready, QT_N * c + k + 1)
                    if k == 0:
                        pe.wait_ge(biased, QT_N * c + 2)
                    for t in range(2):
                        mm = pe.transpose(att_turned(k)[:, P * t:P * (t + 1)], Pr[:, k, TT * t:TT * (t + 1)], m("ident"))
                    mm.then_inc(pt_ready, 1)
                elif step == "attn_apply":
                    pe.wait_ge(pt0_copied, c + 1)
                    pe.wait_ge(pt1_copied, c + 1)
                    for t in range(2):
                        for f in range(2):
                            mm = pe.matmul(bB[HALF[f], 0:T], V[:, t, D * f:D * (f + 1)], PT[:, :, t, D * f:D * (f + 1)],
                                           start=(t == 0), stop=(t == 1))
                    mm.then_inc(pv_ready, 1)
                elif step == "expand":
                    pe.wait_ge(xn_ready[1], c + 1)
                    pe.matmul([bF, bG][k][:, 0:T], m("wiT", HALF[k]), xn[HALF[k], 1, :], start=True, stop=True).then_inc(expand_ready, 1)
                elif step == "experts":
                    l, f = k // 2, k % 2
                    pe.wait_ge(hid_relued, RELUS * c + k + 1)
                    if l == 0:
                        pe.wait_ge(group_selected, GC * c + GC // 2 * (f + 1))
                    if c + k == 0:
                        pe.wait_ge(dve_zeroed, 3)
                    for b in range(2):
                        for j in range(4):
                            g = 4 * b + j
                            mm = pe.matmul([bF, bG][f][COLT * j:COLT * (j + 1), P * b:P * (b + 1)],
                                           hid[:, l, f, RG * g:RG * g + COLT], sel[:, c % 2, GC // 2 * f + g, l, :],
                                           start=True, stop=True, tile_position=(0, COLT * j))
                    mm.then_inc(y_ready, 1)
                elif step == "yturn":
                    pe.wait_ge(yt_ready, 2 * NL * c + k + 1)
                    for b in range(2):
                        mm = pe.transpose([bF, bG][k % 2][:, P * (2 + b):P * (3 + b)], yt[:, k % 2, b, :], m("ident"))
                    mm.then_inc(ytt_ready, 1)
                elif step == "project":
                    pe.wait_ge(hid_relued, RELUS * c + 4 + k + 1)
                    pe.matmul([bF, bG][k][HALF[k], 0:T], m("woT"), hid[:, NL, k, 0:T], start=True, stop=True).then_inc(wo_ready, 1)


def kernel(**inputs):
    import numpy as np
    import concourse.bacc as bacc
    from concourse.bass_utils import run_bass_kernel_spmd

    a = {k: np.asarray(v) for k, v in inputs.items()}
    f32 = np.float32
    x = a["x"].reshape(C, 2, D, 8, 8, 8, 8)
    x = x.transpose(0, 1, 2, 3, 5, 4, 6).reshape(C, P, G, PIX)
    x_ch = np.ascontiguousarray(x.reshape(C, P, G * PIX))
    x_px = np.ascontiguousarray(
        x.reshape(C, P, G // 2, 2, PIX).transpose(0, 3, 4, 2, 1).reshape(C, P, G // 2, P))
    txt = np.ascontiguousarray(a["txt"].reshape(C, 2, TXT, D).transpose(0, 1, 3, 2).reshape(C, P, TXT))

    def twice(v):
        return np.concatenate([v, v], axis=0)

    def put(dst, at, v):
        dst[:v.shape[0], at[0]:at[0] + v.shape[1]] = v

    def diag2(v):
        out = np.zeros((P, P), f32)
        out[:D, :D] = v
        out[D:, D:] = v
        return out

    early = np.zeros((P, EARLY_N), f32)
    put(early, EARLY["wqT"], diag2(a["L0_tok_Wq"].T))
    put(early, EARLY["wk"], diag2(a["L0_tok_Wk"]))
    bk = np.zeros((2, NH, DH, NH, 2, NH), f32)
    for f in range(2):
        for hd in range(NH):
            bk[f, hd, :, :, f, hd] = a["L0_tok_bk"].reshape(NH, DH)[hd][:, None]
    put(early, EARLY["bk"], bk.reshape(P, P))
    put(early, EARLY["bq"], twice(a["L0_tok_bq"])[:, None])
    put(early, EARLY["bv"], twice(a["L0_tok_bv"])[:, None])
    put(early, EARLY["bo"], twice(a["L0_tok_bo"])[:, None])
    put(early, EARLY["head"], twice(np.repeat(np.eye(NH, dtype=f32), DH, axis=0)))
    put(early, EARLY["mask"], np.repeat(np.eye(NH, dtype=f32), SLOT, axis=0))

    mid = np.zeros((P, MID_N), f32)
    put(mid, MID["ident"], np.eye(P, dtype=f32))
    wv = np.zeros((D, NH, COLT // DH, DH), f32)
    for hd in range(NH):
        wv[:, hd, hd % (COLT // DH)] = a["L0_tok_Wv"].T[:, DH * hd:DH * (hd + 1)]
    put(mid, MID["wv_head"], twice(wv.reshape(D, NH * COLT)))
    put(mid, MID["toT"], diag2(a["L0_tok_Wo"].T))
    put(mid, MID["center"], diag2(np.eye(D, dtype=f32) - f32(1.0 / D)))
    put(mid, MID["mean"], diag2(np.full((D, D), 1.0 / D, f32)))
    put(mid, MID["wqT"], diag2(a["L0_attn_Wq"].T))
    put(mid, MID["wkT"], diag2(a["L0_attn_Wk"].T))
    put(mid, MID["wvT"], diag2(a["L0_attn_Wv"].T))
    put(mid, MID["bq"], twice(a["L0_attn_bq"])[:, None])
    put(mid, MID["bk"], twice(a["L0_attn_bk"])[:, None])
    put(mid, MID["bv"], twice(a["L0_attn_bv"])[:, None])
    put(mid, MID["wiT"], twice(a["L0_ffn_Wi"].T))
    put(mid, MID["bi"], a["L0_ffn_bi"][:, None])
    put(mid, MID["woT"], a["L0_ffn_Wo"].T)
    put(mid, MID["bo"], twice(a["L0_ffn_bo"])[:, None])
    br = np.zeros((P, NL, HID), f32)
    br[:NE] = a["L0_ffn_br"].transpose(1, 0, 2)
    br[NE] = a["L0_ffn_bs"][:, 0]
    put(mid, MID["brs"], br.reshape(P, NL * HID))
    rows = np.arange(P)
    put(mid, MID["expert"], np.where(rows < NE, rows, -1).astype(f32)[:, None])
    put(mid, MID["shared"], (rows == NE).astype(f32)[:, None])
    put(mid, MID["beta"], np.broadcast_to(a["L0_attn_beta"], (P, 2)))
    idx = np.arange(T, dtype=f32)
    dist = np.abs(idx[:, None] - idx[None, :])
    cosines = [np.cos(f32(2.0 * np.pi) * dist / f32(t)).astype(f32) for t in (24.0, 720.0)]
    cosines = np.stack(cosines).reshape(2, QT_N, D, T).transpose(2, 0, 1, 3)
    put(mid, MID["wsT"], a["L0_ffn_Ws"][:, 0].transpose(2, 0, 1).reshape(P, NL * HID))

    arrays = {
        "x_ch": x_ch, "x_px": x_px, "txt_ch": txt, "early_in_dram": early, "mid_in_dram": mid,
        "cos_in_dram": twice(cosines),
        "wrT_in": np.ascontiguousarray(a["L0_ffn_Wr"].transpose(3, 1, 0, 2)),
        "route_ids": np.ascontiguousarray(np.broadcast_to(a["L0_ffn_route_id"], (P, 64))),
    }
    nc = bacc.Bacc("TRN2", target_bir_lowering=False, num_devices=1)
    args = [nc.dram_tensor(n, v.shape, mybir.dt.from_np(v.dtype), kind="ExternalInput").ap() for n, v in arrays.items()]
    args.append(nc.dram_tensor("out_dram", (C, P, T), F32, kind="ExternalOutput").ap())
    early_fusion_kernel(nc, *args)
    r = run_bass_kernel_spmd(nc, [arrays], core_ids=[0])
    got = r.results[0]["out_dram"].reshape(C, 2, D, T).transpose(0, 1, 3, 2)
    return np.ascontiguousarray(got.reshape(B, T, D))
```
